# Optimizing a Trainium2 kernel written in Bass

```python
import numpy as np
import jax
import jax.numpy as jnp

def _softmax(x, axis=-1):
    return jax.nn.softmax(x, axis=axis)

def _gelu(x):
    return jax.nn.gelu(x, approximate=True)

def _silu(x):
    return jax.nn.silu(x)

def _sigmoid(x):
    return jax.nn.sigmoid(x)

def _layernorm(x, axis=-1, eps=1e-05):
    m = jnp.mean(x, axis=axis, keepdims=True)
    v = jnp.var(x, axis=axis, keepdims=True)
    return (x - m) / jnp.sqrt(v + eps)

def _scatter_add(tgt, idx, src, axis=0):
    return tgt.at[idx].add(src)

def _segment_sum(src, seg, n):
    return jax.ops.segment_sum(src, seg, n)
kernel_name = 'mk_gnn_resnorm_d2_gnn_r8_f14716'

def setup_inputs(seed: int=0):
    np.random.seed(seed)
    _w = jnp.asarray

    def _rec_inputs():
        import jax
        import jax.numpy as jnp
        _gk = jax.random.key(seed)
        x = -0.0003713 + 1 * jax.random.normal(jax.random.fold_in(_gk, 1), (12500, 128), jnp.float32)
        _s = jax.random.randint(jax.random.fold_in(_gk, 2), (100000,), 0, 12500, jnp.int32)
        _d = jax.random.randint(jax.random.fold_in(_gk, 3), (100000,), 0, 12500, jnp.int32)
        _loop = jnp.arange(12500, dtype=jnp.int32)
        src = jnp.concatenate([_s, _d, _loop])
        dst = jnp.concatenate([_d, _s, _loop])
        _o = jnp.argsort(dst, stable=True)
        src = src[_o]
        dst = dst[_o]
        edge_attr_64 = 0.000135552 + 1.00015 * jax.random.normal(jax.random.fold_in(_gk, 12), (212500, 64), jnp.float32)
        edge_weight = jax.random.uniform(jax.random.fold_in(_gk, 14), (212500,), jnp.float32, 0.0, 999.998)
        node_vec = jax.random.uniform(jax.random.fold_in(_gk, 15), (12500,), jnp.float32, 0.0, 999.994)
        return (x, src, dst, edge_attr_64, edge_weight, node_vec)
    x, src, dst, edge_attr_64, edge_weight, node_vec = _rec_inputs()

    def _L0_gnn_setup():
        import jax, jax.numpy as jnp
        import numpy as np
        import math
        N = 12500
        E = 100000
        IN = 128
        OUT = 128
        MSG = 64
        TDIM = 32
        HEADS = 2
        CH = OUT // HEADS
        EDGE_DIM = MSG + TDIM
        key = jax.random.key(seed)
        ks = jax.random.split(key, 16)
        s = 1.0 / math.sqrt(IN)
        se = 1.0 / math.sqrt(EDGE_DIM)
        return {'x': jax.random.normal(ks[0], (N, IN), jnp.float32), 'last_update': jax.random.uniform(ks[1], (N,), jnp.float32, 0.0, 1000.0), 't': jax.random.uniform(ks[2], (E,), jnp.float32, 0.0, 1000.0), 'msg': jax.random.normal(ks[3], (E, MSG), jnp.float32), 'edge_index': jax.random.randint(ks[4], (2, E), 0, N, jnp.int32), 'time_w': jax.random.normal(ks[5], (TDIM,), jnp.float32), 'time_b': jax.random.normal(ks[6], (TDIM,), jnp.float32) * 0.1, 'Wq': jax.random.normal(ks[7], (IN, OUT), jnp.float32) * s, 'bq': jnp.zeros((OUT,), jnp.float32), 'Wk': jax.random.normal(ks[8], (IN, OUT), jnp.float32) * s, 'bk': jnp.zeros((OUT,), jnp.float32), 'Wv': jax.random.normal(ks[9], (IN, OUT), jnp.float32) * s, 'bv': jnp.zeros((OUT,), jnp.float32), 'We': jax.random.normal(ks[10], (EDGE_DIM, OUT), jnp.float32) * se, 'Wskip': jax.random.normal(ks[11], (IN, OUT), jnp.float32) * s, 'bskip': jnp.zeros((OUT,), jnp.float32)}
    _L0_gnn_all = _L0_gnn_setup()
    _L0_gnn_in = {k: v for k, v in _L0_gnn_all.items() if k in ('time_w', 'time_b', 'Wq', 'bq', 'Wk', 'bk', 'Wv', 'bv', 'We', 'Wskip', 'bskip')}
    del _L0_gnn_all

    def _L1_gnn_setup():
        import jax, jax.numpy as jnp
        import numpy as np
        N = 12500
        E = 80000
        D = 128
        H = 128
        L = 2
        key = jax.random.key(seed)
        ks = jax.random.split(key, 11)
        x = jax.random.normal(ks[0], (N, D), dtype=jnp.float32)
        row = jax.random.randint(ks[1], (E,), 0, N)
        col = jax.random.randint(ks[2], (E,), 0, N)
        s = 1.0 / np.sqrt(H)
        u = lambda k, shape: jax.random.uniform(k, shape, jnp.float32, -s, s)
        gcn_w = u(ks[3], (L, D, H))
        gcn_b = u(ks[4], (L, H))
        nb_w = u(ks[5], (L, D, H))
        nb_b = u(ks[6], (L, H))
        self_w = u(ks[7], (L, D, H))
        self_b = u(ks[8], (L, H))
        att_w = u(ks[9], (L, 2 * H, 1))
        att_b = u(ks[10], (L, 1))
        return dict(x=x, row=row, col=col, gcn_w=gcn_w, gcn_b=gcn_b, nb_w=nb_w, nb_b=nb_b, self_w=self_w, self_b=self_b, att_w=att_w, att_b=att_b)
    _L1_gnn_all = _L1_gnn_setup()
    _L1_gnn_in = {k: v for k, v in _L1_gnn_all.items() if k in ('gcn_w', 'gcn_b', 'nb_w', 'nb_b', 'self_w', 'self_b', 'att_w', 'att_b')}
    del _L1_gnn_all
    return {'x': x, 'src': src, 'dst': dst, 'edge_attr_64': edge_attr_64, 'edge_weight': edge_weight, 'node_vec': node_vec, 'L0_gnn_time_w': _L0_gnn_in['time_w'], 'L0_gnn_time_b': _L0_gnn_in['time_b'], 'L0_gnn_Wq': _L0_gnn_in['Wq'], 'L0_gnn_bq': _L0_gnn_in['bq'], 'L0_gnn_Wk': _L0_gnn_in['Wk'], 'L0_gnn_bk': _L0_gnn_in['bk'], 'L0_gnn_Wv': _L0_gnn_in['Wv'], 'L0_gnn_bv': _L0_gnn_in['bv'], 'L0_gnn_We': _L0_gnn_in['We'], 'L0_gnn_Wskip': _L0_gnn_in['Wskip'], 'L0_gnn_bskip': _L0_gnn_in['bskip'], 'L1_gnn_gcn_w': _L1_gnn_in['gcn_w'], 'L1_gnn_gcn_b': _L1_gnn_in['gcn_b'], 'L1_gnn_nb_w': _L1_gnn_in['nb_w'], 'L1_gnn_nb_b': _L1_gnn_in['nb_b'], 'L1_gnn_self_w': _L1_gnn_in['self_w'], 'L1_gnn_self_b': _L1_gnn_in['self_b'], 'L1_gnn_att_w': _L1_gnn_in['att_w'], 'L1_gnn_att_b': _L1_gnn_in['att_b']}

def reference(x, src, dst, edge_attr_64, edge_weight, node_vec, L0_gnn_time_w, L0_gnn_time_b, L0_gnn_Wq, L0_gnn_bq, L0_gnn_Wk, L0_gnn_bk, L0_gnn_Wv, L0_gnn_bv, L0_gnn_We, L0_gnn_Wskip, L0_gnn_bskip, L1_gnn_gcn_w, L1_gnn_gcn_b, L1_gnn_nb_w, L1_gnn_nb_b, L1_gnn_self_w, L1_gnn_self_b, L1_gnn_att_w, L1_gnn_att_b):
    import jax
    import jax.numpy as jnp

    def _L0_gnn_ref(x, last_update, t, msg, edge_index, time_w, time_b, Wq, bq, Wk, bk, Wv, bv, We, Wskip, bskip):
        import jax, jax.numpy as jnp
        import numpy as np
        import math
        N = 12500
        E = 100000
        IN = 128
        OUT = 128
        MSG = 64
        TDIM = 32
        HEADS = 2
        CH = OUT // HEADS
        EDGE_DIM = MSG + TDIM
        src = edge_index[0]
        dst = edge_index[1]
        rel_t = last_update[src] - t
        rel_t_enc = jnp.cos(rel_t[:, None] * time_w[None, :] + time_b)
        edge_attr = jnp.concatenate([rel_t_enc, msg], axis=-1)
        q_all = x @ Wq + bq
        k_all = x @ Wk + bk
        v_all = x @ Wv + bv
        q = q_all[dst].reshape(-1, HEADS, CH)
        k = k_all[src].reshape(-1, HEADS, CH)
        v = v_all[src].reshape(-1, HEADS, CH)
        e = (edge_attr @ We).reshape(-1, HEADS, CH)
        k = k + e
        alpha = jnp.sum(q * k, axis=-1) / math.sqrt(CH)
        m = jax.ops.segment_max(alpha, dst, num_segments=N)
        m = jnp.where(jnp.isfinite(m), m, 0.0)
        ex = jnp.exp(alpha - m[dst])
        denom = jax.ops.segment_sum(ex, dst, num_segments=N)
        a = ex / (denom[dst] + 1e-16)
        out_e = (v + e) * a[:, :, None]
        out = jax.ops.segment_sum(out_e.reshape(-1, HEADS * CH), dst, num_segments=N)
        out = out + x @ Wskip + bskip
        return out

    def _L1_gnn_ref(x, row, col, gcn_w, gcn_b, nb_w, nb_b, self_w, self_b, att_w, att_b):
        import jax, jax.numpy as jnp
        import numpy as np
        N = 12500
        E = 80000
        D = 128
        H = 128
        L = 2
        leaky = lambda v: jnp.where(v >= 0, v, 0.01 * v)
        h = x
        total = x
        for l in range(L):
            f1 = h[row]
            f2 = h[col]
            a1 = leaky(f1 @ nb_w[l] + nb_b[l])
            a2 = leaky(f2 @ self_w[l] + self_b[l])
            w = jnp.concatenate([a1, a2], axis=1) @ att_w[l] + att_b[l]
            mask = jax.nn.sigmoid(w[:, 0])
            support = h @ gcn_w[l]
            msg = mask[:, None] * support[col]
            out = jax.ops.segment_sum(msg, row, num_segments=N) + gcn_b[l]
            h = jax.nn.relu(out)
            total = total + h
        return total
    edge_index = jnp.stack([src, dst])
    x = _layernorm(x + _L0_gnn_ref(x, node_vec, edge_weight, edge_attr_64, edge_index, L0_gnn_time_w, L0_gnn_time_b, L0_gnn_Wq, L0_gnn_bq, L0_gnn_Wk, L0_gnn_bk, L0_gnn_Wv, L0_gnn_bv, L0_gnn_We, L0_gnn_Wskip, L0_gnn_bskip), axis=-1)
    x = _layernorm(x + _L1_gnn_ref(x, src, dst, L1_gnn_gcn_w, L1_gnn_gcn_b, L1_gnn_nb_w, L1_gnn_nb_b, L1_gnn_self_w, L1_gnn_self_b, L1_gnn_att_w, L1_gnn_att_b), axis=-1)
    return x

_drawn_inputs = setup_inputs


def setup_inputs(seed=0):
    import zlib

    import numpy as np

    out = dict(_drawn_inputs(seed))
    spreads = {'L0_gnn_bq': (0.0, 0.1),
     'L0_gnn_bk': (0.0, 2.0),
     'L0_gnn_bv': (0.0, 0.1),
     'L0_gnn_bskip': (0.0, 0.1)}
    factors = {'L0_gnn_time_b': 3.402, 'L1_gnn_nb_b': 8.0, 'L1_gnn_self_b': 8.0, 'L1_gnn_att_b': 42.67}
    for name, (base, spread) in spreads.items():
        noise = np.random.default_rng([zlib.crc32(name.encode()), seed]).standard_normal(out[name].shape)
        drawn = base * np.exp(spread * noise) if base else spread * noise
        out[name] = jnp.asarray(drawn.astype(out[name].dtype))
    for name, factor in factors.items():
        out[name] = (out[name] * factor).astype(out[name].dtype)
    return out
```

```python
from contextlib import ExitStack

import concourse.bass as bass
from concourse import mybir

F32 = mybir.dt.float32
BF16 = mybir.dt.bfloat16
I32 = mybir.dt.int32
U32 = mybir.dt.uint32
ALU = mybir.AluOpType
ACT = mybir.ActivationFunctionType
AX = mybir.AxisListType

P = 128
N, D = 12500, 128
E = 212500
HEADS, CH = 2, 64
MSG, TDIM = 64, 32
LAYERS = 2
NB = -(-N // P)
FULL = N // P
REST = N - FULL * P
EP, EC = 125, E // 125
STREAMS = 5
STEPS = EC // STREAMS
BINS = STREAMS * NB
MAX_TILES = -(-((E + NB * (P - 1)) // P) // 16) * 16
QUADS = MAX_TILES // 4
GROUP = 8
TBL = MAX_TILES + 16
NEG = -1e30
KV = 2 * D + 1
LR = D + 1
R0 = 4 + MSG
R0E = R0 + TDIM
R1 = 2
HW = CH + 1
SB = 7
NSTEP = NB // SB
EPS = 1e-5
TWO_PI_HI = 6.28125
TWO_PI_LO = 0.0019353071795864769
INV_TWO_PI = 0.15915494309189535
MAGIC = 12582912.0
HALF_PI = 1.5707963267948966

assert EP * EC == E and STEPS * STREAMS == EC and NSTEP * SB == NB and STEPS % 4 == 0


def is_loop(q):
    return not isinstance(q, int)


def run_steps(eng, peel, total, body):
    for q in range(peel):
        body(q, q % 4)
    fours = (total - peel) // 4
    with eng.Fori(0, fours) as i:
        for r in range(4):
            body(4 * i + (peel + r), (peel + r) % 4)
    for q in range(peel + 4 * fours, total):
        body(q, q % 4)


def turns(eng, peel, total, body):
    for i in range(peel):
        body(i)
    with eng.Fori(peel, total) as i:
        body(i)


def wait_used(eng, sem, value):
    if is_loop(value) or value > 0:
        eng.wait_ge(sem, value)


class Chain:

    def __init__(self, eng, sem, base):
        self.eng, self.sem, self.base, self.n = eng, sem, base, 0

    def then(self, instruction):
        instruction.then_inc(self.sem, 1)
        self.n += 1
        self.eng.wait_ge(self.sem, self.base + self.n)


def semaphores(nc, stack, prefix):
    taken = []

    def take(name):
        taken.append(nc.alloc_semaphore(prefix + name))
        return taken[-1]

    def give_back():
        nc.all_engine_barrier()
        nc.clear_and_free_semaphores(taken)
        nc.all_engine_barrier()

    stack.callback(give_back)
    return take


def build(nc, a, out):
    top = ExitStack()
    with top:
        def dram(name, shape, dt):
            return nc.dram_tensor(name, shape, dt, kind="Internal").ap()

        kvtab = dram("kvtab", [NB * P, KV], F32)
        ltab = [dram(f"ltab{l}", [NB * P, LR], F32) for l in range(LAYERS)]
        rec0 = dram("rec0", [MAX_TILES * P, R0], F32)
        rec1 = dram("rec1", [MAX_TILES * P, R1], F32)
        btab = [dram("bucket_of_tile0", [TBL], I32), dram("bucket_of_tile1", [TBL], I32)]

        def sb(name, shape, dt, stack=top):
            return stack.enter_context(nc.sbuf_tensor(name, shape, dt))

        c = dict(
            iota=sb("iota", [P, P], F32), icol=sb("icol", [P, 1], F32), ident=sb("ident", [P, P], F32),
            ones=sb("ones", [P, P], F32), half_pi=sb("half_pi", [P, 1], F32), eps=sb("eps", [P, 1], F32),
        )
        regA = sb("regA", [P, NB, D], F32)
        acc = sb("acc", [P, NB, HEADS * HW], F32)

        constants(nc, c)
        with ExitStack() as st:
            xall = sb("x_phase1", [P, NB, D], F32, st)
            node_tables(nc, st, a, c, xall, regA, kvtab, rec0, rec1, acc)
        for key in range(2):
            with ExitStack() as st:
                bin_edges(nc, st, a, c, key, rec0 if key == 0 else rec1, btab[key])
        with ExitStack() as st:
            attention(nc, st, a, c, regA, acc, kvtab, rec0, btab[0])
        with ExitStack() as st:
            xall = sb("x_res", [P, NB, D], F32, st)
            with ExitStack() as s2:
                node_stage(nc, s2, a, c, "attn", 0, xall, regA, acc, ltab, out)
            for l in range(LAYERS):
                with ExitStack() as s2:
                    convolution(nc, s2, c, l, regA, acc, ltab[l], rec1, btab[1])
                with ExitStack() as s2:
                    last = l == LAYERS - 1
                    node_stage(nc, s2, a, c, "last" if last else "mid", l + 1, xall, regA, acc, ltab, out)


def constants(nc, c):
    with ExitStack() as st:
        ii = st.enter_context(nc.sbuf_tensor("ii", [P, P], I32))
        ic = st.enter_context(nc.sbuf_tensor("ic", [P, 1], I32))
        sem = semaphores(nc, st, "i_")
        iota_ready, cast_ready = sem("iota_ready"), sem("cast_ready")
        block = st.enter_context(nc.Block())

        @block.gpsimd
        def _(pool):
            nc.gpsimd.iota(ii[:], [[1, P]], base=0, channel_multiplier=0).then_inc(iota_ready, 1)
            nc.gpsimd.iota(ic[:], [[0, 1]], base=0, channel_multiplier=1).then_inc(iota_ready, 1)

        @block.vector
        def _(dve):
            nc.vector.memset(c["ones"][:], 1.0)
            nc.vector.memset(c["half_pi"][:], HALF_PI)
            nc.vector.memset(c["eps"][:], EPS)
            dve.wait_ge(iota_ready, 2)
            nc.vector.tensor_copy(c["iota"][:], ii[:])
            nc.vector.tensor_copy(c["icol"][:], ic[:]).then_inc(cast_ready, 1)
            dve.wait_ge(cast_ready, 1)
            nc.vector.tensor_scalar(c["ident"][:], c["iota"][:], c["icol"][:, 0:1], None, ALU.is_equal)


def load_nodes(eng, x, dst, sem):
    one = x.shape[1] == 1
    eng.dma_start(dst[:, 0:FULL, :], x[0:FULL * P, :].rearrange("(b p) d -> p b d", p=P),
                  allow_slow_non_contiguous=one).then_inc(sem, 16)
    eng.dma_start(dst[0:REST, FULL, :], x[FULL * P:N, :]).then_inc(sem, 16)


def node_tables(nc, st, a, c, xall, q_all, kvtab, rec0, rec1, acc):
    def sb(name, shape, dt=F32):
        return st.enter_context(nc.sbuf_tensor("n_" + name, shape, dt))

    sem = semaphores(nc, st, "n_")

    w = sb("w", [P, 3, D])
    bias = sb("bias", [P, 3, D])
    nv = sb("nv", [P, NB, 1])
    xs = sb("xs", [P, SB, D])
    xT = sb("xT", [P, SB, D])
    kv = sb("kv", [P, SB, KV])
    fill0 = sb("fill0", [P, GROUP, R0])
    fill1 = sb("fill1", [P, MAX_TILES, R1])
    psT = st.enter_context(nc.psum_tensor("n_psT", [P, 1024], F32))
    ps = [st.enter_context(nc.psum_tensor(f"n_ps{k}", [P, 1024], F32)) for k in range(3)]
    zeroed, loaded, small, filled, stored0 = sem("zeroed"), sem("loaded"), sem("small"), sem("filled"), sem("stored0")
    bias_ready = sem("bias_ready")
    xs_ready, turned, xT_ready, products = sem("xs_ready"), sem("turned"), sem("xT_ready"), sem("products")
    nv_ready, kv_ready, kv_stored, q_ready = sem("nv_ready"), sem("kv_ready"), sem("kv_stored"), sem("q_ready")
    block = st.enter_context(nc.Block())

    @block.sync
    def _(sp):
        sp.wait_ge(zeroed, 1)
        load_nodes(sp, a["x"], xall, loaded)
        load_nodes(sp, a["node_vec"].rearrange("(n o) -> n o", o=1), nv, loaded)
        for k, n in enumerate("qkv"):
            sp.dma_start(w[:, k, :], a[f"L0_gnn_W{n}"]).then_inc(small, 16)
            sp.dma_start(bias[:, k, :], a[f"L0_gnn_b{n}"].rearrange("(o d) -> o d", o=1).broadcast_to([P, D])).then_inc(small, 16)
        kvt = kvtab.rearrange("(b p) d -> p b d", p=P)
        with sp.Fori(0, NSTEP) as i:
            sp.wait_ge(kv_ready, i + 1)
            sp.dma_start(kvt[:, bass.ds(i * SB, SB), :], kv[:]).then_inc(kv_stored, 16)
        sp.wait_ge(kv_stored, 16 * NSTEP)

    @block.gpsimd
    def _(pool):
        nc.gpsimd.memset(xall[:, FULL, :], 0.0)
        nc.gpsimd.memset(nv[:, FULL, :], 0.0).then_inc(zeroed, 1)
        nc.gpsimd.memset(fill0[:], 0.0).then_inc(filled, 1)
        nc.gpsimd.memset(fill1[:], 0.0).then_inc(filled, 1)
        pool.wait_ge(filled, 2)
        nc.gpsimd.memset(fill0[:, :, 2], -1.0).then_inc(filled, 1)
        nc.gpsimd.memset(fill1[:, :, 1], -1.0).then_inc(filled, 1)
        nc.gpsimd.memset(acc[:], 0.0)

    @block.scalar
    def _(act):
        act.wait_ge(filled, 4)
        act.dma_start(rec1.rearrange("(p t) d -> p t d", p=P), fill1[:]).then_inc(stored0, 16)
        r0 = rec0.rearrange("(g p t) d -> p g (t d)", p=P, t=GROUP)
        half = MAX_TILES // GROUP // 4
        for k in range(4):
            act.dma_start(r0[:, k * half:(k + 1) * half, :],
                          fill0[:].rearrange("p t d -> p (t d)").unsqueeze(1).broadcast_to([P, half, GROUP * R0])).then_inc(stored0, 16)
        act.wait_ge(loaded, 64)

        def turn(i):
            wait_used(act, turned, i)
            nc.scalar.copy(xs[:], xall[:, bass.ds(i * SB, SB), :]).then_inc(xs_ready, 1)
            wait_used(act, kv_stored, 16 * i)
            nc.scalar.copy(kv[:, :, 2 * D:KV], nv[:, bass.ds(i * SB, SB), :]).then_inc(nv_ready, 1)

        turns(act, 1, NSTEP, turn)
        act.wait_ge(stored0, 80)

    @block.tensor
    def _(pe):
        pe.wait_ge(small, 96)

        def turn(i):
            pe.wait_ge(xs_ready, i + 1)
            wait_used(pe, xT_ready, i)
            for j in range(SB):
                m = nc.tensor.transpose(psT[:, j * D:(j + 1) * D], xs[:, j, :], c["ident"][:])
            m.then_inc(turned, 1)
            pe.wait_ge(xT_ready, i + 1)
            wait_used(pe, kv_ready, i)
            wait_used(pe, q_ready, i)
            for k in range(3):
                for j in range(SB):
                    m = nc.tensor.matmul(ps[k][:, j * D:(j + 1) * D], xT[:, j, :], w[:, k, :], start=True, stop=True)
            m.then_inc(products, 1)

        turns(pe, 1, NSTEP, turn)

    @block.vector
    def _(dve):
        dve.wait_ge(small, 96)
        nc.vector.tensor_scalar(bias[:, 0, :], bias[:, 0, :], CH ** -0.5, None, ALU.mult).then_inc(bias_ready, 1)
        dve.wait_ge(bias_ready, 1)

        def turn(i):
            dve.wait_ge(turned, i + 1)
            wait_used(dve, products, i)
            nc.vector.tensor_copy(xT[:].rearrange("p b d -> p (b d)"), psT[:, 0:SB * D]).then_inc(xT_ready, 1)
            dve.wait_ge(products, i + 1)

            def view(k):
                return ps[k][:, 0:SB * D].rearrange("p (b d) -> p b d", d=D)

            def bb(k):
                return bias[:, k, :].unsqueeze(1).broadcast_to([P, SB, D])

            nc.vector.scalar_tensor_tensor(q_all[:, bass.ds(i * SB, SB), :], view(0), CH ** -0.5, bb(0),
                                           ALU.mult, ALU.add).then_inc(q_ready, 1)
            wait_used(dve, kv_stored, 16 * i)
            nc.vector.tensor_tensor(kv[:, :, 0:D], view(1), bb(1), ALU.add)
            dve.wait_ge(nv_ready, i + 1)
            nc.vector.tensor_tensor(kv[:, :, D:2 * D], view(2), bb(2), ALU.add).then_inc(kv_ready, 1)

        turns(dve, 1, NSTEP, turn)


def bin_edges(nc, st, a, c, key, rec, btab):
    pre = f"b{key}_"

    def sb(name, shape, dt=F32):
        return st.enter_context(nc.sbuf_tensor(pre + name, shape, dt))

    sem = semaphores(nc, st, pre)

    keys = sb("keys", [EP, EC], I32)
    other = sb("other", [EP, EC], I32)
    times = sb("times", [EP, EC], F32) if key == 0 else None
    tmp = sb("tmp", [EP, EC], I32)
    bucket = sb("bucket", [EP, EC], BF16)
    place = sb("place", [EP, EC], F32)
    iota_b = sb("iota_b", [EP, NB], BF16)
    before = sb("before", [EP, EP], BF16)
    rest = sb("rest", [EP, EP], BF16)
    ones_b = sb("ones_b", [EP, EP], BF16)
    hot = [sb(f"hot{k}", [EP, STREAMS, NB], BF16) for k in range(2)]
    cnt = sb("cnt", [EP, STREAMS, NB])
    start = sb("start", [EP, STREAMS, NB])
    bins = sb("bins", [EP, 4, NB])
    tiles_i = sb("tiles_i", [EP, NB], I32)
    tcols = TBL // 111
    tid_i = sb("tid_i", [111, tcols], I32)
    tid = sb("tid", [111, tcols])
    ended = sb("ended", [111, tcols, NB])
    bt = sb("bt", [111, tcols])
    bt_i = sb("bt_i", [111, tcols], I32)
    hit = sb("hit", [EP, STREAMS, NB])
    posf = sb("posf", [EP, STREAMS])
    pos = sb("pos", [EP, 4, STREAMS], I32)
    slot = [sb(f"slot{k}", [EP, STREAMS], I32) for k in range(4)]
    width = R0 if key == 0 else R1
    recs = [sb(f"recs{k}", [EP, STREAMS, width]) for k in range(4)]
    ps_cnt = st.enter_context(nc.psum_tensor(pre + "ps_cnt", [P, 512], F32))
    ps_pos = st.enter_context(nc.psum_tensor(pre + "ps_pos", [P, 512], F32))
    assert 111 * tcols == TBL

    edges_in, prep, tid_ready = sem("edges_in"), sem("prep"), sem("tid_ready")
    hot_ready, hot_used, prep_done = sem("hot_ready"), sem("hot_used"), sem("prep_done")
    start_ready, table_ready, table_stored = sem("start_ready"), sem("table_ready"), sem("table_stored")
    hot2_ready, rank_ready, rank_read = sem("hot2_ready"), sem("rank_ready"), sem("rank_read")
    turn_begun = sem("turn_begun")
    pos_step, slot_ready, payload_ready = sem("pos_step"), sem("slot_ready"), sem("payload_ready")
    message_in = [sem(f"message_in{k}") for k in range(4)]
    scattered = [sem(f"scattered{k}") for k in range(4)]
    quarter = STEPS // 4
    block = st.enter_context(nc.Block())

    def cols(t, q):
        return t[:, bass.ds(q * STREAMS, STREAMS)]

    @block.sync
    def _(sp):
        names = ("dst", "src") if key == 0 else ("src", "dst")
        sp.dma_start(keys[:], a[names[0]].rearrange("(p c) -> p c", p=EP)).then_inc(edges_in, 16)
        sp.dma_start(other[:], a[names[1]].rearrange("(p c) -> p c", p=EP)).then_inc(edges_in, 16)
        if key == 0:
            sp.dma_start(times[:], a["edge_weight"].rearrange("(p c) -> p c", p=EP)).then_inc(edges_in, 16)
            msgs = a["edge_attr_64"].rearrange("(p c) d -> p c d", p=EP)

            def turn(i):
                for u in range(4):
                    wait_used(sp, scattered[u], 16 * STREAMS * i)
                    sp.dma_start(recs[u][:, :, 4:R0], msgs[:, bass.ds((4 * i + u) * STREAMS, STREAMS), :]).then_inc(message_in[u], 16)

            turns(sp, 1, quarter, turn)
        sp.wait_ge(table_ready, 1)
        sp.dma_start(btab.rearrange("(p c) -> p c", p=111), bt_i[:]).then_inc(table_stored, 16)
        sp.wait_ge(table_stored, 16)

    @block.gpsimd
    def _(pool):
        nc.gpsimd.iota(tid_i[:], [[1, tcols]], base=0, channel_multiplier=tcols).then_inc(tid_ready, 1)
        if key == 0:
            for k in range(4):
                m = nc.gpsimd.memset(recs[k][:, :, 3], 0.0)
            m.then_inc(tid_ready, 1)
            pool.wait_ge(tid_ready, 2)
        with pool.Fori(0, quarter) as i:
            for u in range(4):
                pool.wait_ge(slot_ready, 4 * i + (u + 1))
                pool.wait_ge(payload_ready, 4 * i + (u + 1))
                if key == 0:
                    pool.wait_ge(message_in[u], 16 * i + 16)
                pool.sem_inc(turn_begun, 1)
                for j in range(STREAMS):
                    nc.gpsimd.indirect_dma_start(
                        out=rec, out_offset=bass.IndirectOffsetOnAxis(slot[u][:, j:j + 1].bitcast(U32), 0),
                        in_=recs[u][:, j, :], in_offset=None).then_inc(scattered[u], 16)
        for u in range(4):
            pool.wait_ge(scattered[u], 16 * STREAMS * quarter)

    @block.scalar
    def _(act):
        act.wait_ge(edges_in, 48 if key == 0 else 32)
        act.wait_ge(prep_done, 1)

        def turn(i):
            for u in range(4):
                wait_used(act, scattered[u], 16 * STREAMS * i)
                q = 4 * i + u
                ri = recs[u][:].bitcast(I32)
                if key == 0:
                    nc.scalar.copy(recs[u][:, :, 0], cols(times, q))
                    nc.scalar.copy(ri[:, :, 1], cols(other, q))
                    m = nc.scalar.copy(recs[u][:, :, 2], cols(place, q))
                else:
                    nc.scalar.copy(ri[:, :, 0], cols(other, q))
                    m = nc.scalar.copy(recs[u][:, :, 1], cols(place, q))
                m.then_inc(payload_ready, 1)

        turns(act, 1, quarter, turn)

    @block.tensor
    def _(pe):
        pe.wait_ge(prep_done, 1)
        nc.tensor.matmul(ps_cnt[0:EP, 0:BINS], ones_b[:], hot[1][:].rearrange("p s b -> p (s b)"), start=True, stop=True).then_inc(hot_used, 1)
        with pe.Fori(0, quarter) as i:
            for u in range(4):
                pe.wait_ge(hot_ready, 4 * i + (u + 1))
                nc.tensor.matmul(ps_cnt[0:EP, 0:BINS], ones_b[:], hot[u % 2][:].rearrange("p s b -> p (s b)"),
                                 start=False, stop=True, skip_group_check=True).then_inc(hot_used, 1)
        pe.wait_ge(start_ready, 1)
        nc.tensor.matmul(ps_pos[0:EP, 0:BINS], c["ones"][0:1, 0:EP], start[0:1, :, :].rearrange("p s b -> p (s b)"), start=True, stop=True)
        with pe.Fori(0, quarter) as i:
            for u in range(4):
                h = hot[u % 2][:].rearrange("p s b -> p (s b)")
                pe.wait_ge(hot2_ready, 4 * i + (u + 1))
                nc.tensor.matmul(ps_pos[0:EP, 0:BINS], before[:], h, start=False, stop=True, skip_group_check=True).then_inc(rank_ready, 1)
                pe.wait_ge(rank_read, 4 * i + (u + 1))
                nc.tensor.matmul(ps_pos[0:EP, 0:BINS], rest[:], h, start=False, stop=True, skip_group_check=True)

    @block.vector
    def _(dve):
        dve.wait_ge(edges_in, 48 if key == 0 else 32)
        ch = Chain(dve, prep, 0)
        ch.then(nc.vector.tensor_scalar(tmp[:], keys[:], 7, None, ALU.logical_shift_right))
        ch.then(nc.vector.tensor_copy(bucket[:], tmp[:]))
        ch.then(nc.vector.tensor_scalar(tmp[:], keys[:], P - 1, None, ALU.bitwise_and))
        nc.vector.tensor_copy(place[:], tmp[:])
        nc.vector.tensor_copy(iota_b[:], c["iota"][0:EP, 0:NB])
        nc.vector.tensor_scalar(before[:], c["iota"][0:EP, 0:EP], c["icol"][0:EP, 0:1], None, ALU.is_gt)
        nc.vector.tensor_scalar(rest[:], c["iota"][0:EP, 0:EP], c["icol"][0:EP, 0:1], None, ALU.is_le)
        nc.vector.memset(ones_b[:], 1.0)
        ch.then(nc.vector.memset(hot[1][:], 0.0))
        dve.sem_inc(prep_done, 1)

        def one_hot(k, q):
            return nc.vector.tensor_tensor(
                hot[k][:], cols(bucket, q).unsqueeze(2).broadcast_to([EP, STREAMS, NB]),
                iota_b[:].unsqueeze(1).broadcast_to([EP, STREAMS, NB]), ALU.is_equal)

        def count(i):
            for u in range(4):
                wait_used(dve, hot_used, 4 * i + u)
                one_hot(u % 2, 4 * i + u).then_inc(hot_ready, 1)

        turns(dve, 1, quarter, count)
        dve.wait_ge(hot_used, STEPS + 1)
        ch.then(nc.vector.tensor_copy(cnt[:].rearrange("p s b -> p (s b)"), ps_cnt[0:EP, 0:BINS]))
        ch.then(nc.vector.tensor_reduce(bins[:, 0, :], cnt[:].rearrange("p s b -> p b s"), AX.X, ALU.add))
        ch.then(nc.vector.tensor_scalar(bins[:, 1, :], bins[:, 0, :], float(P - 1), None, ALU.add))
        ch.then(nc.vector.tensor_copy(tiles_i[:], bins[:, 1, :]))
        ch.then(nc.vector.tensor_scalar(tiles_i[:], tiles_i[:], 7, None, ALU.logical_shift_right))
        ch.then(nc.vector.tensor_copy(bins[:, 1, :], tiles_i[:]))
        ch.then(nc.vector.memset(bins[:, 3, :], 0.0))
        ch.then(nc.vector.tensor_tensor_scan(bins[:, 2, :], bins[:, 1, :], bins[:, 3, :], 0.0, ALU.add, ALU.add))
        ch.then(nc.vector.tensor_tensor(bins[:, 3, :], bins[:, 2, :], bins[:, 1, :], ALU.subtract))
        ch.then(nc.vector.tensor_scalar(start[:, 0, :], bins[:, 3, :], float(P), None, ALU.mult))
        for s in range(1, STREAMS):
            ch.then(nc.vector.tensor_tensor(start[:, s, :], start[:, s - 1, :], cnt[:, s - 1, :], ALU.add))
        dve.sem_inc(start_ready, 1)
        dve.wait_ge(tid_ready, 1)
        ch.then(nc.vector.tensor_copy(tid[:], tid_i[:]))
        ch.then(nc.vector.tensor_tensor(ended[:], bins[0:111, 2, :].unsqueeze(1).broadcast_to([111, tcols, NB]),
                                        tid[:].unsqueeze(2).broadcast_to([111, tcols, NB]), ALU.is_le))
        ch.then(nc.vector.tensor_reduce(bt[:], ended[:], AX.X, ALU.add))
        nc.vector.tensor_scalar(bt_i[:], bt[:], float(NB - 1), None, ALU.min).then_inc(table_ready, 1)

        def rank(i):
            for u in range(4):
                q = 4 * i + u
                one_hot(u % 2, q).then_inc(hot2_ready, 1)
                dve.wait_ge(hot2_ready, q + 1)
                dve.wait_ge(rank_ready, q + 1)
                nc.vector.tensor_tensor(hit[:].rearrange("p s b -> p (s b)"), hot[u % 2][:].rearrange("p s b -> p (s b)"),
                                        ps_pos[0:EP, 0:BINS], ALU.mult).then_inc(rank_read, 1)
                dve.wait_ge(rank_read, q + 1)
                cs = Chain(dve, pos_step, 16 * i + 4 * u)
                cs.then(nc.vector.tensor_reduce(posf[:], hit[:], AX.X, ALU.add))
                cs.then(nc.vector.tensor_copy(pos[:, 0, :], posf[:]))
                if key == 0:
                    nc.vector.tensor_scalar(pos[:, 1, :], pos[:, 0, :], P - 1, 3, ALU.bitwise_and, ALU.logical_shift_left)
                    cs.then(nc.vector.tensor_scalar(pos[:, 2, :], pos[:, 0, :], 7, GROUP - 1, ALU.logical_shift_right, ALU.bitwise_and))
                    nc.vector.tensor_scalar(pos[:, 3, :], pos[:, 0, :], ~(P * GROUP - 1), None, ALU.bitwise_and)
                    cs.then(nc.vector.tensor_tensor(pos[:, 1, :], pos[:, 1, :], pos[:, 2, :], ALU.bitwise_or))
                    wait_used(dve, scattered[u], 16 * STREAMS * i)
                    nc.vector.tensor_tensor(slot[u][:], pos[:, 1, :], pos[:, 3, :], ALU.bitwise_or).then_inc(slot_ready, 1)
                else:
                    cs.then(nc.vector.tensor_scalar(pos[:, 1, :], pos[:, 0, :], P - 1, None, ALU.bitwise_and))
                    cs.then(nc.vector.tensor_scalar(pos[:, 2, :], pos[:, 0, :], 7, None, ALU.logical_shift_right))
                    wait_used(dve, scattered[u], 16 * STREAMS * i)
                    nc.vector.scalar_tensor_tensor(slot[u][:], pos[:, 1, :], float(MAX_TILES), pos[:, 2, :],
                                                   ALU.mult, ALU.add).then_inc(slot_ready, 1)
                assert cs.n == 4

        turns(dve, 1, quarter, rank)


def attention(nc, st, a, c, q_all, acc, kvtab, rec0, btab):
    def sb(name, shape, dt=F32):
        return st.enter_context(nc.sbuf_tensor("a_" + name, shape, dt))

    sem = semaphores(nc, st, "a_")

    def ps(name, width=512):
        return st.enter_context(nc.psum_tensor("a_" + name, [P, width], F32))

    we = sb("we", [MSG + TDIM, D])
    tw = sb("tw", [P, TDIM])
    tb = sb("tb", [P, TDIM])
    brow = sb("brow", [1, TBL], I32)
    ball = sb("ball", [P, TBL], I32)
    pen = sb("pen", [P, TBL])
    rec = [sb(f"rec{k}", [P, GROUP, R0E]) for k in range(2)]
    g = [sb(f"g{k}", [P, 4, KV]) for k in range(4)]
    hot = [sb(f"hot{k}", [P, 4, P]) for k in range(4)]
    miss = [sb(f"miss{k}", [P, 4, P]) for k in range(4)]
    hotT = [sb(f"hotT{k}", [P, 4 * P]) for k in range(4)]
    eaT = [sb(f"eaT{k}", [MSG + TDIM, 4 * P]) for k in range(2)]
    rel = sb("rel", [P, GROUP])
    arg = sb("arg", [P, GROUP, TDIM])
    cyc = sb("cyc", [P, GROUP, TDIM])
    zz = sb("zz", [P, GROUP, TDIM])
    za = sb("za", [P, GROUP, TDIM])
    kk = sb("kk", [P, 4, D])
    qk = sb("qk", [P, 4, D])
    vv = [sb(f"vv{k}", [P, 4, D]) for k in range(2)]
    score = [sb(f"score{k}", [P, 4, HEADS]) for k in range(2)]
    sc = sb("sc", [P, 4, HEADS, P])
    tmax = sb("tmax", [P, 4, HEADS])
    mx = [sb(f"mx{k}", [P, 5, HEADS]) for k in range(2)]
    old = sb("old", [P, 4, HEADS])
    penq = [sb(f"penq{k}", [P, 4]) for k in range(4)]
    dd = [sb(f"dd{k}", [P, 2, 4, HEADS]) for k in range(2)]
    ex = [sb(f"ex{k}", [P, 2, 4, HEADS]) for k in range(2)]
    wv = [sb(f"wv{k}", [P, 4, HEADS, HW]) for k in range(2)]
    psT, psE, psM, psQ = ps("psT"), ps("psE"), ps("psM"), ps("psQ")
    psX, psA = ps("psX", 1024), ps("psA", 1024)

    small, table_in, pen_step, pen_ready, turn_begun = sem("small"), sem("table_in"), sem("pen_step"), sem("pen_ready"), sem("turn_begun")
    rec_in = [sem(f"rec_in{k}") for k in range(2)]
    gathered = [sem(f"gathered{k}") for k in range(4)]
    miss_ready, hot_ready, angle_ready, enc_ready = sem("miss_ready"), sem("hot_ready"), sem("angle_ready"), sem("enc_ready")
    ea_turned, eaT_ready, hot_turned, hotT_ready = sem("ea_turned"), sem("eaT_ready"), sem("hot_turned"), sem("hotT_ready")
    e_ready, qg_ready, vv_ready, qk_ready, sc_ready = sem("e_ready"), sem("qg_ready"), sem("vv_ready"), sem("qk_ready"), sem("sc_ready")
    sc_turned, tmax_ready, mx_ready, m_ready, dd_ready = sem("sc_turned"), sem("tmax_ready"), sem("mx_ready"), sem("m_ready"), sem("dd_ready")
    ex_ready, wv_ready, sum_ready, added, pen_in = sem("ex_ready"), sem("wv_ready"), sem("sum_ready"), sem("added"), sem("pen_in")
    enc_step, abs_ready, score_ready, mx_step = sem("enc_step"), sem("abs_ready"), sem("score_ready"), sem("mx_step")
    block = st.enter_context(nc.Block())

    def sums(i):
        at = 512 * (i // 2) + (i % 2) * HEADS * HW
        return psA[:, at:at + HEADS * HW]

    def front_of(q):
        return q // 2 + 1 if isinstance(q, int) else None

    groups = QUADS // 2
    TOTAL = QUADS + 2

    def fronts(q, r):
        if r % 2:
            return None
        if isinstance(q, int):
            f = q // 2 + 1
            return (f, f % 2) if f < groups else None
        return ("loop", (r // 2 + 1) % 2)

    def steps(eng, body, lead=None):
        if lead:
            lead(0, 0)
        fours = (QUADS - 2) // 4
        for q in range(2):
            body(q, q % 4, (q // 2 + 1) if q % 2 == 0 else None)
        with eng.Fori(0, fours) as i:
            for r in range(4):
                body(4 * i + (2 + r), (2 + r) % 4, (2 * i + (2 + r // 2)) if r % 2 == 0 else None)
        for q in range(2 + 4 * fours, TOTAL):
            f = q // 2 + 1
            body(q, q % 4, f if q % 2 == 0 and f < groups else None)

    def live(q):
        return is_loop(q) or 0 <= q < QUADS

    def load_in(q, slots):
        return q

    @block.sync
    def _(sp):
        sp.dma_start(we[0:MSG, :], a["L0_gnn_We"][TDIM:TDIM + MSG, :]).then_inc(small, 16)
        sp.dma_start(we[MSG:MSG + TDIM, :], a["L0_gnn_We"][0:TDIM, :]).then_inc(small, 16)
        sp.dma_start(tw[:], a["L0_gnn_time_w"].rearrange("(o d) -> o d", o=1).broadcast_to([P, TDIM])).then_inc(small, 16)
        sp.dma_start(tb[:], a["L0_gnn_time_b"].rearrange("(o d) -> o d", o=1).broadcast_to([P, TDIM])).then_inc(small, 16)
        sp.dma_start(brow[:], btab.rearrange("(o d) -> o d", o=1)).then_inc(table_in, 16)
        sp.dma_start(ball[:], btab.rearrange("(o d) -> o d", o=1).broadcast_to([P, TBL])).then_inc(table_in, 16)
        r0 = rec0.rearrange("(g p t) d -> g p t d", p=P, t=GROUP)

        def load(f, s):
            sp.dma_start(rec[s][:, :, 0:R0], r0[bass.ds(f, 1), :, :, :].rearrange("o p t d -> (o p) t d")).then_inc(rec_in[s], 16)

        load(0, 0)
        load(1, 1)

        def reload(f, s):
            sp.wait_ge(ea_turned, 2 * f - 2)
            sp.wait_ge(hot_ready, 2 * f - 2)
            load(f, s)

        with sp.Fori(0, (groups - 2) // 2) as i:
            reload(2 * i + 2, 0)
            reload(2 * i + 3, 1)

    @block.gpsimd
    def _(pool):
        def front(f, s, k, loop):
            pool.wait_ge(rec_in[s], 16 * k + 16)
            for h in range(2):
                r = 2 * s + h
                if loop:
                    pool.wait_ge(vv_ready, 2 * f + (h - 3))
                pool.sem_inc(turn_begun, 1)
                for j in range(4):
                    idx = rec[s][:, 4 * h + j, 1:2].bitcast(U32)
                    nc.gpsimd.indirect_dma_start(out=g[r][:, j, :], out_offset=None, in_=kvtab,
                                                 in_offset=bass.IndirectOffsetOnAxis(idx, 0)).then_inc(gathered[r], 16)

        front(0, 0, 0, False)
        front(1, 1, 0, False)
        with pool.Fori(0, (groups - 2) // 2) as i:
            front(2 * i + 2, 0, i + 1, True)
            front(2 * i + 3, 1, i + 1, True)

    @block.scalar
    def _(act):
        def front(f, s, q, first):
            act.wait_ge(angle_ready, f + 1)
            nc.scalar.activation(za[:], zz[:], ACT.Abs).then_inc(abs_ready, 1)
            act.wait_ge(abs_ready, f + 1)
            nc.scalar.activation(rec[s][:, :, R0:R0E], za[:], ACT.Sin, bias=c["half_pi"][:, 0:1], scale=-1.0).then_inc(enc_ready, 1)
            for h in range(2):
                r = 2 * s + h
                act.wait_ge(ea_turned, 2 * f + (h + 1))
                if not first:
                    act.wait_ge(e_ready, 2 * f + (h - 1))
                nc.scalar.copy(eaT[h][:], psT[0:MSG + TDIM, :]).then_inc(eaT_ready, 1)

        def turned_hot(q, r):
            act.wait_ge(hot_turned, q + 1)
            nc.scalar.copy(hotT[r][:], psT[:]).then_inc(hotT_ready, 1)
            nc.scalar.activation(miss[r][:], hot[r][:], ACT.Copy, bias=NEG, scale=-NEG).then_inc(miss_ready, 1)

        def masked(q, r):
            act.wait_ge(score_ready, q + 1)
            act.wait_ge(miss_ready, q + 1)
            wait_used(act, sc_turned, q)
            for j in range(4):
                for h in range(HEADS):
                    m = nc.scalar.activation(sc[:, j, h, :], miss[r][:, j, :], ACT.Identity, bias=score[r % 2][:, j, h:h + 1], scale=1.0)
            m.then_inc(sc_ready, 1)

        def body(q, r, f):
            if live(q):
                masked(q, r)
            if live(q - 1):
                wait_used(act, dd_ready, q)
                nc.scalar.activation(ex[(r - 1) % 2][:], dd[(r - 1) % 2][:], ACT.Exp).then_inc(ex_ready, 1)
            if f is not None:
                front(f, (r // 2 + 1) % 2, q, False)
            if live(q + 2):
                turned_hot(q + 2, (r + 2) % 4)

        front(0, 0, 0, True)
        turned_hot(0, 0)
        turned_hot(1, 1)
        steps(act, body)

    @block.tensor
    def _(pe):
        def front(f, s):
            for h in range(2):
                r = 2 * s + h
                if h == 0:
                    pe.wait_ge(enc_ready, f + 1)
                if h == 0:
                    wait_used(pe, hotT_ready, 2 * f)
                else:
                    pe.wait_ge(eaT_ready, 2 * f + 1)
                for j in range(4):
                    m = nc.tensor.transpose(psT[0:MSG + TDIM, j * P:(j + 1) * P], rec[s][:, 4 * h + j, 4:R0E], c["ident"][:])
                m.then_inc(ea_turned, 1)

        def turn_hot(q, r):
            pe.wait_ge(hot_ready, q + 1)
            if r % 2 == 0:
                pe.wait_ge(eaT_ready, q + 2)
            else:
                pe.wait_ge(hotT_ready, q)
            for j in range(4):
                m = nc.tensor.transpose(psT[:, j * P:(j + 1) * P], hot[r][:, j, :], c["ident"][:])
            m.then_inc(hot_turned, 1)

        def edge_and_query(q, r):
            pe.wait_ge(eaT_ready, q + 1)
            wait_used(pe, vv_ready, q)
            for j in range(4):
                m = nc.tensor.matmul(psE[:, j * D:(j + 1) * D], eaT[r % 2][:, j * P:(j + 1) * P], we[:], start=True, stop=True)
            m.then_inc(e_ready, 1)
            pe.wait_ge(hotT_ready, q + 1)
            wait_used(pe, qk_ready, q)
            _, bs = nc.values_load_multi_w_load_instructions(brow[0:1, bass.ds(4 * q, 4)], engines=[mybir.EngineType.PE],
                                                             min_val=0, max_val=NB - 1, skip_runtime_bounds_check_because="the table is clamped to the last bucket")
            for j in range(4):
                m = nc.tensor.matmul(psQ[:, j * D:(j + 1) * D], hotT[r][:, j * P:(j + 1) * P], q_all[:, bass.ds(bs[j], 1), :].rearrange("p o d -> p (o d)"),
                                     start=True, stop=True)
            m.then_inc(qg_ready, 1)

        def body(q, r, f):
            if live(q - 1):
                p = (r - 1) % 4
                wait_used(pe, mx_ready, q)
                for j in range(4):
                    m = nc.tensor.matmul(psM[:, 2 * j:2 * j + 2], hotT[p][:, j * P:(j + 1) * P], mx[p % 2][:, j + 1, :], start=True, stop=True)
                m.then_inc(m_ready, 1)
            if live(q + 1):
                edge_and_query(q + 1, (r + 1) % 4)
            if live(q):
                pe.wait_ge(sc_ready, q + 1)
                wait_used(pe, tmax_ready, q)
                for j in range(4):
                    for h in range(HEADS):
                        m = nc.tensor.transpose(psX[:, (2 * j + h) * P:(2 * j + h + 1) * P], sc[:, j, h, :], c["ident"][:])
                m.then_inc(sc_turned, 1)
            if live(q - 1):
                wait_used(pe, wv_ready, q)
                for j in range(4):
                    m = nc.tensor.matmul(sums(j), hot[p][:, j, :], wv[p % 2][:, j, :, :].rearrange("p h w -> p (h w)"), start=True, stop=True)
                m.then_inc(sum_ready, 1)
            if f is not None:
                front(f, (r // 2 + 1) % 2)
            if live(q + 2):
                turn_hot(q + 2, (r + 2) % 4)

        pe.wait_ge(small, 64)
        pe.wait_ge(table_in, 32)
        front(0, 0)
        turn_hot(0, 0)
        turn_hot(1, 1)
        edge_and_query(0, 0)
        steps(pe, body)

    @block.vector
    def _(dve):
        def front(f, s, k, q):
            for h in range(2):
                r = 2 * s + h
                dve.wait_ge(gathered[r], 64 * k + 64)
                m = nc.vector.tensor_tensor(rel[:, 4 * h:4 * h + 4], g[r][:, :, 2 * D], rec[s][:, 4 * h:4 * h + 4, 0], ALU.subtract)
            cs = Chain(dve, enc_step, 6 * f)
            cs.then(m)
            tw_b = tw[:].unsqueeze(1).broadcast_to([P, GROUP, TDIM])
            cs.then(nc.vector.tensor_tensor(arg[:], rel[:].unsqueeze(2).broadcast_to([P, GROUP, TDIM]), tw_b, ALU.mult))
            cs.then(nc.vector.tensor_tensor(arg[:], arg[:], tb[:].unsqueeze(1).broadcast_to([P, GROUP, TDIM]), ALU.add))
            cs.then(nc.vector.tensor_scalar(cyc[:], arg[:], INV_TWO_PI, MAGIC, ALU.mult, ALU.add))
            cs.then(nc.vector.tensor_scalar(cyc[:], cyc[:], MAGIC, None, ALU.subtract))
            cs.then(nc.vector.scalar_tensor_tensor(arg[:], cyc[:], -TWO_PI_HI, arg[:], ALU.mult, ALU.add))
            wait_used(dve, enc_ready, f)
            nc.vector.scalar_tensor_tensor(zz[:], cyc[:], -TWO_PI_LO, arg[:], ALU.mult, ALU.add).then_inc(angle_ready, 1)

        def one_hot(q, r):
            if is_loop(q) or q >= 4:
                dve.wait_ge(sum_ready, q - 3)
            h = r % 2
            nc.vector.tensor_tensor(hot[r][:], rec[r // 2][:, 4 * h:4 * h + 4, 2:3].broadcast_to([P, 4, P]),
                                    c["iota"][:].unsqueeze(1).broadcast_to([P, 4, P]), ALU.is_equal).then_inc(hot_ready, 1)

        def scores(q, r):
            e4 = psE[:].rearrange("p (t d) -> p t d", d=D)
            dve.wait_ge(e_ready, q + 1)
            nc.vector.tensor_tensor(kk[:], e4, g[r][:, :, 0:D], ALU.add)
            if is_loop(q) or q >= 2:
                dve.wait_ge(wv_ready, q - 1)
            nc.vector.tensor_tensor(vv[r % 2][:], e4, g[r][:, :, D:2 * D], ALU.add).then_inc(vv_ready, 1)
            dve.wait_ge(vv_ready, q + 1)
            dve.wait_ge(qg_ready, q + 1)
            nc.vector.tensor_tensor(qk[:], kk[:], psQ[:].rearrange("p (t d) -> p t d", d=D), ALU.mult).then_inc(qk_ready, 1)
            dve.wait_ge(qk_ready, q + 1)
            nc.vector.tensor_reduce(score[r % 2][:].rearrange("p t h -> p (t h)"), qk[:].rearrange("p t (h d) -> p (t h) d", h=HEADS),
                                    AX.X, ALU.add).then_inc(score_ready, 1)

        def maxima(q, r):
            m_, prev = mx[r % 2], mx[(r + 1) % 2]
            cs = Chain(dve, mx_step, 5 * q)
            nc.vector.tensor_copy(penq[r][:], pen[:, bass.ds(4 * q, 4)])
            cs.then(nc.vector.tensor_copy(m_[:, 0, :], prev[:, 4, :]))
            dve.wait_ge(sc_turned, q + 1)
            nc.vector.tensor_reduce(tmax[:].rearrange("p t h -> p (t h)"), psX[:].rearrange("p (t d) -> p t d", d=P), AX.X, ALU.max).then_inc(tmax_ready, 1)
            dve.wait_ge(tmax_ready, q + 1)
            for h in range(HEADS):
                m = nc.vector.tensor_tensor_scan(m_[:, 1:5, h], penq[r][:], tmax[:, :, h], m_[:, 0, h:h + 1], ALU.add, ALU.max)
            m.then_inc(mx_ready, 1)

        def exponents(q, r):
            m_ = mx[r % 2]
            cs = Chain(dve, mx_step, 5 * q + 1)
            dve.wait_ge(mx_ready, q + 1)
            cs.then(nc.vector.tensor_tensor(old[:], m_[:, 0:4, :], penq[r][:].unsqueeze(2).broadcast_to([P, 4, HEADS]), ALU.add))
            cs.then(nc.vector.tensor_tensor(dd[r % 2][:, 1, :, :], old[:], m_[:, 1:5, :], ALU.subtract))
            dve.wait_ge(m_ready, q + 1)
            cs.then(nc.vector.tensor_tensor(dd[r % 2][:, 0, :, :].rearrange("p t h -> p (t h)"), score[r % 2][:].rearrange("p t h -> p (t h)"),
                                            psM[:, 0:8], ALU.subtract))
            cs.then(nc.vector.tensor_scalar(dd[r % 2][:, 0, :, :], dd[r % 2][:, 0, :, :], 0.0, None, ALU.min))
            dve.sem_inc(dd_ready, 1)

        def weigh(q, r):
            dve.wait_ge(ex_ready, q + 1)
            e = ex[r % 2][:, 0, :, :]
            nc.vector.tensor_tensor(wv[r % 2][:, :, :, 0:CH], vv[r % 2][:].rearrange("p t (h d) -> p t h d", h=HEADS),
                                    e.unsqueeze(3).broadcast_to([P, 4, HEADS, CH]), ALU.mult)
            nc.vector.tensor_copy(wv[r % 2][:, :, :, CH], e).then_inc(wv_ready, 1)

        def add(q, r):
            dve.wait_ge(table_in, 32)
            _, bs = nc.values_load_multi_w_load_instructions(brow[0:1, bass.ds(4 * q, 4)], engines=[mybir.EngineType.DVE],
                                                             min_val=0, max_val=NB - 1, skip_runtime_bounds_check_because="the table is clamped to the last bucket")
            dve.wait_ge(sum_ready, q + 1)
            for j in range(4):
                for h in range(HEADS):
                    n = HEADS * j + h
                    dve.wait_ge(added, 8 * q + max(n, 1))
                    at = acc[:, bass.ds(bs[j], 1), h * HW:(h + 1) * HW].rearrange("p o w -> p (o w)")
                    nc.vector.scalar_tensor_tensor(at, at, ex[r % 2][:, 1, j, h:h + 1], sums(j)[:, h * HW:(h + 1) * HW],
                                                   ALU.mult, ALU.add).then_inc(added, 1)

        def body(q, r, f):
            if live(q):
                scores(q, r)
            if live(q - 1):
                maxima(q - 1, (r - 1) % 4)
            if live(q - 2):
                add(q - 2, (r - 2) % 4)
            if live(q - 1):
                exponents(q - 1, (r - 1) % 4)
            if f is not None:
                s = (r // 2 + 1) % 2
                front(f, s, f // 2 if isinstance(f, int) else (f - s) // 2, q)
            if live(q + 2):
                one_hot(q + 2, (r + 2) % 4)
            if live(q - 1):
                weigh(q - 1, (r - 1) % 4)

        dve.wait_ge(small, 64)
        dve.wait_ge(table_in, 32)
        cp = Chain(dve, pen_step, 0)
        nc.vector.memset(mx[1][:], NEG)
        cp.then(nc.vector.tensor_copy(pen[:], ball[:]))
        cp.then(nc.vector.tensor_tensor(pen[:, 1:TBL], ball[:, 1:TBL], ball[:, 0:TBL - 1], ALU.not_equal))
        cp.then(nc.vector.memset(pen[:, 0:1], 1.0))
        cp.then(nc.vector.tensor_scalar(pen[:], pen[:], NEG, None, ALU.mult))
        dve.sem_inc(pen_ready, 1)
        dve.sem_inc(added, 1)
        front(0, 0, 0, 0)
        one_hot(0, 0)
        one_hot(1, 1)
        steps(dve, body)


def node_stage(nc, st, a, c, kind, layer, xall, s1_all, acc, ltab, out):
    pre = f"s{layer}_"

    def sb(name, shape, dt=F32):
        return st.enter_context(nc.sbuf_tensor(pre + name, shape, dt))

    sem = semaphores(nc, st, pre)

    prepare = kind != "last"
    W = [P, SB, D]
    r_, h_ = sb("r", W), sb("h", W)
    sq = sb("sq", W)
    st_ = sb("stats", [P, 4, SB])
    biases = sb("biases", [P, 6, D])
    if kind == "attn":
        xs, wskip, den = sb("xs", W), sb("wskip", [P, D]), sb("den", [P, 2, SB, HEADS])
        bneed = [("L0_gnn_bskip", None)]
    else:
        bneed = [("L1_gnn_gcn_b", layer - 1)]
    if prepare:
        w = sb("w", [P, 3, D])
        hT, dg, trow, s1 = sb("hT", W), sb("dg", W), sb("trow", [P, SB, LR]), sb("s1", [P, 2, SB])
        attb = sb("attb", [P, 1])
        zeros = sb("zeros", [P, SB, HEADS * HW])
    psT = st.enter_context(nc.psum_tensor(pre + "psT", [P, 1024], F32))
    ps = [st.enter_context(nc.psum_tensor(pre + f"ps{k}", [P, 1024], F32)) for k in range(3)]

    def view(t):
        return t[:, 0:SB * D].rearrange("p (b d) -> p b d", d=D)

    def row(k):
        return biases[:, k, :].unsqueeze(1).broadcast_to(W)

    small, xin, x_copied, x_turned, skip_ready = sem("small"), sem("xin"), sem("x_copied"), sem("x_turned"), sem("skip_ready")
    step, var_ready, sd_ready, h_ready, h_turned = sem("step"), sem("var_ready"), sem("sd_ready"), sem("h_ready"), sem("h_turned")
    xT_ready, hT_ready, products, s1_ready, dg_ready = sem("xT_ready"), sem("hT_ready"), sem("products"), sem("s1_ready"), sem("dg_ready")
    spread, spread_read, support_ready, stored, s2_ready = sem("spread"), sem("spread_read"), sem("support_ready"), sem("stored"), sem("s2_ready")
    zeroed, tail_zeroed = sem("zeroed"), sem("tail_zeroed")
    block = st.enter_context(nc.Block())
    nsmall = 0

    @block.sync
    def _(sp):
        def vec(dst, src):
            sp.dma_start(dst, src.broadcast_to(list(dst.shape))).then_inc(small, 16)

        if kind == "attn":
            sp.wait_ge(tail_zeroed, 1)
            load_nodes(sp, a["x"], xall, xin)
            vec(biases[:, 0, :], a["L0_gnn_bskip"].rearrange("(o d) -> o d", o=1))
            sp.dma_start(wskip[:], a["L0_gnn_Wskip"]).then_inc(small, 16)
        else:
            vec(biases[:, 0, :], a["L1_gnn_gcn_b"][layer - 1:layer, :])
            vec(biases[:, 5, :], a["L1_gnn_gcn_b"][layer - 1:layer, :])
        if prepare:
            for k, n in enumerate(("nb", "self", "gcn")):
                sp.dma_start(w[:, k, :], a[f"L1_gnn_{n}_w"][layer]).then_inc(small, 16)
            vec(biases[:, 1, :], a["L1_gnn_nb_b"][layer:layer + 1, :])
            vec(biases[:, 2, :], a["L1_gnn_self_b"][layer:layer + 1, :])
            vec(biases[:, 3, :], a["L1_gnn_att_w"][layer, 0:D, :].rearrange("d o -> o d"))
            vec(biases[:, 4, :], a["L1_gnn_att_w"][layer, D:2 * D, :].rearrange("d o -> o d"))
            vec(attb[:], a["L1_gnn_att_b"][layer:layer + 1, :])
            lt = ltab[layer].rearrange("(b p) d -> p b d", p=P)
            with sp.Fori(0, NSTEP) as i:
                sp.wait_ge(s2_ready, i + 1)
                sp.wait_ge(support_ready, i + 1)
                sp.dma_start(lt[:, bass.ds(i * SB, SB), :], trow[:]).then_inc(stored, 16)
            sp.wait_ge(stored, 16 * NSTEP)
        else:
            sp.wait_ge(h_ready, NSTEP)
            sp.dma_start(out[0:FULL * P, :].rearrange("(b p) d -> p b d", p=P), xall[:, 0:FULL, :]).then_inc(stored, 16)
            sp.dma_start(out[FULL * P:N, :], xall[0:REST, FULL, :]).then_inc(stored, 16)
            sp.wait_ge(stored, 32)

    SMALL = 16 * (2 + (8 if prepare else 0))

    @block.gpsimd
    def _(pool):
        if kind == "attn":
            nc.gpsimd.memset(xall[:, FULL, :], 0.0).then_inc(tail_zeroed, 1)
        if prepare:
            nc.gpsimd.memset(zeros[:], 0.0).then_inc(zeroed, 1)

    @block.scalar
    def _(act):
        if kind == "attn":
            act.wait_ge(xin, 32)

        def turn(i):
            if kind == "attn":
                wait_used(act, h_ready, i)
                nc.scalar.copy(xs[:], xall[:, bass.ds(i * SB, SB), :]).then_inc(x_copied, 1)
            if kind != "mid":
                act.wait_ge(var_ready, i + 1)
                nc.scalar.activation(st_[:, 3, :], st_[:, 2, :], ACT.Sqrt, bias=c["eps"][:, 0:1], scale=1.0 / D).then_inc(sd_ready, 1)
            if prepare:
                act.wait_ge(products, i + 1)
                wait_used(act, stored, 16 * i)
                nc.scalar.copy(trow[:, :, 0:D], view(ps[2])).then_inc(support_ready, 1)
                act.wait_ge(spread, i + 1)
                nc.scalar.copy(s1_all[:, bass.ds(i * SB, SB), :], view(psT)).then_inc(spread_read, 1)

        turns(act, 1, NSTEP, turn)

    @block.tensor
    def _(pe):
        if not prepare:
            return
        pe.wait_ge(small, SMALL)

        def turn(i):
            wait_used(pe, spread_read, i)
            if kind == "attn":
                pe.wait_ge(x_copied, i + 1)
                for j in range(SB):
                    m = nc.tensor.transpose(psT[:, j * D:(j + 1) * D], xs[:, j, :], c["ident"][:])
                m.then_inc(x_turned, 1)
                pe.wait_ge(xT_ready, i + 1)
                for j in range(SB):
                    m = nc.tensor.matmul(ps[0][:, j * D:(j + 1) * D], hT[:, j, :], wskip[:], start=True, stop=True)
                m.then_inc(skip_ready, 1)
            pe.wait_ge(h_ready, i + 1)
            for j in range(SB):
                m = nc.tensor.transpose(psT[:, j * D:(j + 1) * D], h_[:, j, :], c["ident"][:])
            m.then_inc(h_turned, 1)
            pe.wait_ge(hT_ready, i + 1)
            wait_used(pe, support_ready, i)
            for k in range(3):
                for j in range(SB):
                    m = nc.tensor.matmul(ps[k][:, j * D:(j + 1) * D], hT[:, j, :], w[:, k, :], start=True, stop=True)
            m.then_inc(products, 1)
            pe.wait_ge(dg_ready, i + 1)
            for j in range(SB):
                m = nc.tensor.matmul(psT[:, j * D:(j + 1) * D], c["ones"][:], dg[:, j, :], start=True, stop=True)
            m.then_inc(spread, 1)

        turns(pe, 1, NSTEP, turn)

    @block.vector
    def _(dve):
        dve.wait_ge(small, SMALL)
        if prepare:
            dve.wait_ge(zeroed, 1)
        K = {"attn": 19, "mid": 9, "last": 8}[kind]

        def turn(i):
            cs = Chain(dve, step, K * i)
            here = bass.ds(i * SB, SB)

            def norm(final):
                cs.then(nc.vector.tensor_reduce(st_[:, 0, :], r_[:], AX.X, ALU.add))
                cs.then(nc.vector.tensor_scalar(st_[:, 1, :], st_[:, 0, :], 1.0 / D, None, ALU.mult))
                cs.then(nc.vector.tensor_tensor(r_[:], r_[:], st_[:, 1, :].unsqueeze(2).broadcast_to(W), ALU.subtract))
                cs.then(nc.vector.tensor_tensor(sq[:], r_[:], r_[:], ALU.mult))
                nc.vector.tensor_reduce(st_[:, 2, :], sq[:], AX.X, ALU.add).then_inc(var_ready, 1)
                dve.wait_ge(sd_ready, i + 1)
                cs.then(nc.vector.reciprocal(st_[:, 0, :], st_[:, 3, :]))
                nc.vector.tensor_tensor(final, r_[:], st_[:, 0, :].unsqueeze(2).broadcast_to(W), ALU.mult).then_inc(h_ready, 1)
                dve.wait_ge(h_ready, i + 1)

            if kind == "attn":
                cs.then(nc.vector.tensor_scalar(den[:, 0, :, :], acc[:, here, CH::HW], 1e-16, None, ALU.add))
                cs.then(nc.vector.reciprocal(den[:, 1, :, :], den[:, 0, :, :]))
                cs.then(nc.vector.tensor_tensor(
                    sq[:].rearrange("p b (h d) -> p b h d", h=HEADS),
                    acc[:, here, :].rearrange("p b (h w) -> p b h w", h=HEADS)[:, :, :, 0:CH],
                    den[:, 1, :, :].unsqueeze(3).broadcast_to([P, SB, HEADS, CH]), ALU.mult))
                dve.wait_ge(x_turned, i + 1)
                nc.vector.tensor_copy(hT[:].rearrange("p b d -> p (b d)"), psT[:, 0:SB * D]).then_inc(xT_ready, 1)
                dve.wait_ge(skip_ready, i + 1)
                cs.then(nc.vector.tensor_tensor(r_[:], view(ps[0]), row(0), ALU.add))
                cs.then(nc.vector.tensor_tensor(r_[:], r_[:], sq[:], ALU.add))
                dve.wait_ge(x_copied, i + 1)
                cs.then(nc.vector.tensor_tensor(r_[:], r_[:], xs[:], ALU.add))
                norm(h_[:])
                nc.vector.tensor_scalar(xall[:, here, :], h_[:], 2.0, None, ALU.mult)
            else:
                cs.then(nc.vector.tensor_tensor(r_[:], acc[:, here, 0:D], row(0), ALU.add))
                if kind == "mid":
                    nc.vector.tensor_scalar(h_[:], r_[:], 0.0, None, ALU.max).then_inc(h_ready, 1)
                    dve.wait_ge(h_ready, i + 1)
                    nc.vector.tensor_tensor(xall[:, here, :], xall[:, here, :], h_[:], ALU.add)
                else:
                    cs.then(nc.vector.tensor_scalar(r_[:], r_[:], 0.0, None, ALU.max))
                    cs.then(nc.vector.tensor_tensor(r_[:], r_[:], xall[:, here, :], ALU.add))
                    norm(xall[:, here, :])
            if prepare:
                nc.vector.tensor_copy(acc[:, here, :], zeros[:])
                dve.wait_ge(h_turned, i + 1)
                nc.vector.tensor_copy(hT[:].rearrange("p b d -> p (b d)"), psT[:, 0:SB * D]).then_inc(hT_ready, 1)
                dve.wait_ge(products, i + 1)
                for k in range(2):
                    cs.then(nc.vector.tensor_tensor(sq[:], view(ps[k]), row(1 + k), ALU.add))
                    cs.then(nc.vector.scalar_tensor_tensor(sq[:], sq[:], 0.01, sq[:], ALU.mult, ALU.max))
                    cs.then(nc.vector.tensor_tensor(sq[:], sq[:], row(3 + k), ALU.mult))
                    if k == 0:
                        cs.then(nc.vector.tensor_reduce(s1[:, 0, :], sq[:], AX.X, ALU.add))
                        nc.vector.tensor_tensor(dg[:], c["ident"][:].unsqueeze(1).broadcast_to(W),
                                                s1[:, 0, :].unsqueeze(2).broadcast_to(W), ALU.mult).then_inc(dg_ready, 1)
                    else:
                        cs.then(nc.vector.tensor_reduce(s1[:, 1, :], sq[:], AX.X, ALU.add))
                wait_used(dve, stored, 16 * i)
                nc.vector.tensor_scalar(trow[:, :, D], s1[:, 1, :], attb[:, 0:1], None, ALU.add).then_inc(s2_ready, 1)
            assert cs.n == K, (kind, cs.n)

        turns(dve, 1, NSTEP, turn)


def convolution(nc, st, c, layer, s1_all, acc, ltab, rec1, btab):
    pre = f"c{layer}_"

    def sb(name, shape, dt=F32):
        return st.enter_context(nc.sbuf_tensor(pre + name, shape, dt))

    sem = semaphores(nc, st, pre)

    brow = sb("brow", [1, TBL], I32)
    records = sb("records", [P, MAX_TILES, R1])
    rec = [sb(f"rec{k}", [P, 4, R1]) for k in range(4)]
    g = [sb(f"g{k}", [P, 4, LR]) for k in range(4)]
    junk = sb("junk", [P, 8, P])
    z = [sb(f"z{k}", [P, 4]) for k in range(2)]
    gate_in = [sb(f"gate_in{k}", [P, 4]) for k in range(2)]
    gate = [sb(f"gate{k}", [P, 4]) for k in range(2)]
    hot = [sb(f"hot{k}", [P, 4, P]) for k in range(2)]
    psA = [st.enter_context(nc.psum_tensor(pre + f"psA{k}", [P, 512], F32)) for k in range(2)]
    table_in, records_in, rec_ready, turn_begun = sem("table_in"), sem("records_in"), sem("rec_ready"), sem("turn_begun")
    gathered = [sem(f"gathered{k}") for k in range(4)]
    z_ready, gate_in_ready, gate_ready, hot_ready, sum_ready, added = (
        sem("z_ready"), sem("gate_in_ready"), sem("gate_ready"), sem("hot_ready"), sem("sum_ready"), sem("added"))
    block = st.enter_context(nc.Block())

    @block.sync
    def _(sp):
        sp.dma_start(records[:], rec1.rearrange("(p t) d -> p t d", p=P)).then_inc(records_in, 16)
        sp.dma_start(brow[:], btab.rearrange("(o d) -> o d", o=1)).then_inc(table_in, 16)

    @block.gpsimd
    def _(pool):
        def body(q, r):
            pool.wait_ge(rec_ready, q + 1)
            if is_loop(q) or q >= 4:
                pool.wait_ge(sum_ready, q - 3)
            pool.sem_inc(turn_begun, 1)
            for j in range(4):
                nc.gpsimd.indirect_dma_start(out=g[r][:, j, :], out_offset=None, in_=ltab,
                                             in_offset=bass.IndirectOffsetOnAxis(rec[r][:, j, 0:1].bitcast(U32), 0)).then_inc(gathered[r], 16)

        run_steps(pool, 4, QUADS, body)

    @block.scalar
    def _(act):
        def take(q, r):
            nc.scalar.copy(rec[r][:], records[:, bass.ds(4 * q, 4), :]).then_inc(rec_ready, 1)

        def body(q, r):
            act.wait_ge(gate_in_ready, q + 1)
            nc.scalar.activation(gate[r % 2][:], gate_in[r % 2][:], ACT.Sigmoid).then_inc(gate_ready, 1)
            if is_loop(q) or q + 4 < QUADS:
                act.wait_ge(hot_ready, q + 1)
                take(q + 4, r)

        act.wait_ge(records_in, 16)
        for q in range(4):
            take(q, q)
        last = QUADS - 4
        with act.Fori(0, last // 4) as i:
            for r in range(4):
                body(4 * i + r, r)
        for q in range(last, QUADS):
            body(q, q % 4)

    @block.tensor
    def _(pe):
        def body(q, r):
            pe.wait_ge(hot_ready, q + 1)
            if is_loop(q) or q >= 2:
                pe.wait_ge(added, 4 * q - 3)
            for j in range(4):
                m = nc.tensor.matmul(psA[r % 2][:, j * D:(j + 1) * D], hot[r % 2][:, j, :], g[r][:, j, 0:D], start=True, stop=True)
            m.then_inc(sum_ready, 1)

        run_steps(pe, 2, QUADS, body)

    @block.vector
    def _(dve):
        def buckets(q):
            dve.wait_ge(table_in, 16)
            _, bs = nc.values_load_multi_w_load_instructions(brow[0:1, bass.ds(4 * q, 4)], engines=[mybir.EngineType.DVE],
                                                             min_val=0, max_val=NB - 1, skip_runtime_bounds_check_because="the table is clamped to the last bucket")
            return bs

        def gates(q, r, k):
            bs = buckets(q)
            dve.wait_ge(gathered[r], 64 * k + 64)
            for j in range(4):
                s1 = s1_all[:, bass.ds(bs[j], 1), :].rearrange("p o d -> p (o d)")
                m = nc.vector.scalar_tensor_tensor(junk[:, 4 * (r % 2) + j, :], c["iota"][:], rec[r][:, j, 1:2], s1,
                                                   ALU.is_equal, ALU.mult, accum_out=z[r % 2][:, j:j + 1])
            m.then_inc(z_ready, 1)
            dve.wait_ge(z_ready, q + 1)
            nc.vector.tensor_tensor(gate_in[r % 2][:], z[r % 2][:], g[r][:, :, D], ALU.add).then_inc(gate_in_ready, 1)

        def body(q, r, k):
            if is_loop(q) or q < QUADS:
                gates(q, r, k)
            spreads = is_loop(q) or 1 <= q <= QUADS
            adds = is_loop(q) or q >= 2
            if adds:
                bs = buckets(q - 2)
                dve.wait_ge(sum_ready, q - 1)
            if spreads:
                dve.wait_ge(gate_ready, q)
            for j in range(4):
                if adds:
                    dve.wait_ge(added, 4 * (q - 2) + (j + 1))
                    at = acc[:, bass.ds(bs[j], 1), 0:D].rearrange("p o d -> p (o d)")
                    nc.vector.tensor_tensor(at, at, psA[r % 2][:, j * D:(j + 1) * D], ALU.add).then_inc(added, 1)
                if spreads:
                    p = (r - 1) % 4
                    m = nc.vector.tensor_scalar(hot[p % 2][:, j, :], c["iota"][:], rec[p][:, j, 1:2],
                                                gate[p % 2][:, j:j + 1], ALU.is_equal, ALU.mult)
            if spreads:
                m.then_inc(hot_ready, 1)

        dve.wait_ge(table_in, 16)
        dve.sem_inc(added, 1)
        for q in range(2):
            body(q, q, 0)
        fours = (QUADS - 2) // 4
        with dve.Fori(0, fours) as i:
            for r in range(4):
                body(4 * i + (2 + r), (2 + r) % 4, i if r < 2 else i + 1)
        for q in range(2 + 4 * fours, QUADS + 2):
            body(q, q % 4, q // 4)


_INS = ["x", "src", "dst", "edge_attr_64", "edge_weight", "node_vec"] + [
    f"L0_gnn_{n}" for n in ("time_w", "time_b", "Wq", "bq", "Wk", "bk", "Wv", "bv", "We", "Wskip", "bskip")] + [
    f"L1_gnn_{n}" for n in ("gcn_w", "gcn_b", "nb_w", "nb_b", "self_w", "self_b", "att_w", "att_b")]


def kernel(**inputs):
    import numpy as _np
    import concourse.bacc as _bacc
    from concourse import mybir as _mybir
    from concourse.bass_utils import run_bass_kernel_spmd as _run

    nc = _bacc.Bacc("TRN2", target_bir_lowering=False, num_devices=1)
    arrays, args = {}, {}
    for name in _INS:
        arr = _np.ascontiguousarray(inputs[name])
        arrays[f"in_{name}"] = arr
        args[name] = nc.dram_tensor(f"in_{name}", arr.shape, _mybir.dt.from_np(arr.dtype), kind="ExternalInput").ap()
    out = nc.dram_tensor("out", (N, D), _mybir.dt.float32, kind="ExternalOutput").ap()
    build(nc, args, out)
    r = _run(nc, [arrays], core_ids=[0])
    return r.results[0]["out"]
```

```python
from contextlib import ExitStack

import concourse.bass as bass
from concourse import mybir

F32 = mybir.dt.float32
BF16 = mybir.dt.bfloat16
I32 = mybir.dt.int32
U32 = mybir.dt.uint32
ALU = mybir.AluOpType
ACT = mybir.ActivationFunctionType
AX = mybir.AxisListType

P = 128
N, D = 12500, 128
E = 212500
HEADS, CH = 2, 64
MSG, TDIM = 64, 32
LAYERS = 2
NB = -(-N // P)
FULL = N // P
REST = N - FULL * P
EP, EC = 125, E // 125
STREAMS = 5
STEPS = EC // STREAMS
BINS = STREAMS * NB
MAX_TILES = -(-((E + NB * (P - 1)) // P) // 16) * 16
QUADS = MAX_TILES // 4
GROUP = 8
TBL = MAX_TILES + 16
NEG = -1e30
KV = 2 * D + 1
LR = D + 1
R0 = 4 + MSG
R0E = R0 + TDIM
R1 = 2
HW = CH + 1
SB = 7
NSTEP = NB // SB
EPS = 1e-5
TWO_PI_HI = 6.28125
TWO_PI_LO = 0.0019353071795864769
INV_TWO_PI = 0.15915494309189535
MAGIC = 12582912.0
HALF_PI = 1.5707963267948966

assert EP * EC == E and STEPS * STREAMS == EC and NSTEP * SB == NB and STEPS % 4 == 0


def is_loop(q):
    return not isinstance(q, int)


def run_steps(eng, peel, total, body):
    for q in range(peel):
        body(q, q % 4)
    fours = (total - peel) // 4
    with eng.Fori(0, fours) as i:
        for r in range(4):
            body(4 * i + (peel + r), (peel + r) % 4)
    for q in range(peel + 4 * fours, total):
        body(q, q % 4)


def turns(eng, peel, total, body):
    for i in range(peel):
        body(i)
    with eng.Fori(peel, total) as i:
        body(i)


def wait_used(eng, sem, value):
    if is_loop(value) or value > 0:
        eng.wait_ge(sem, value)


class Chain:

    def __init__(self, eng, sem, base):
        self.eng, self.sem, self.base, self.n = eng, sem, base, 0

    def then(self, instruction):
        instruction.then_inc(self.sem, 1)
        self.n += 1
        self.eng.wait_ge(self.sem, self.base + self.n)


def semaphores(nc, stack, prefix):
    taken = []

    def take(name):
        taken.append(nc.alloc_semaphore(prefix + name))
        return taken[-1]

    def give_back():
        nc.all_engine_barrier()
        nc.clear_and_free_semaphores(taken)
        nc.all_engine_barrier()

    stack.callback(give_back)
    return take


def build(nc, a, out):
    top = ExitStack()
    with top:
        def dram(name, shape, dt):
            return nc.dram_tensor(name, shape, dt, kind="Internal").ap()

        kvtab = dram("kvtab", [NB * P, KV], F32)
        ltab = [dram(f"ltab{l}", [NB * P, LR], F32) for l in range(LAYERS)]
        rec0 = dram("rec0", [MAX_TILES * P, R0], F32)
        rec1 = dram("rec1", [MAX_TILES * P, R1], F32)
        btab = [dram("bucket_of_tile0", [TBL], I32), dram("bucket_of_tile1", [TBL], I32)]

        def sb(name, shape, dt, stack=top):
            return stack.enter_context(nc.sbuf_tensor(name, shape, dt))

        c = dict(
            iota=sb("iota", [P, P], F32), icol=sb("icol", [P, 1], F32), ident=sb("ident", [P, P], F32),
            ones=sb("ones", [P, P], F32), half_pi=sb("half_pi", [P, 1], F32), eps=sb("eps", [P, 1], F32),
        )
        regA = sb("regA", [P, NB, D], F32)
        acc = sb("acc", [P, NB, HEADS * HW], F32)

        constants(nc, c)
        with ExitStack() as st:
            xall = sb("x_phase1", [P, NB, D], F32, st)
            node_tables(nc, st, a, c, xall, regA, kvtab, rec0, rec1, acc)
        with ExitStack() as both:
            late = sb("late", [EP, EC, 3], I32, both)
            with ExitStack() as st:
                bin_edges(nc, st, a, c, late, rec0, btab)
            with ExitStack() as st:
                attention(nc, st, a, c, regA, acc, kvtab, rec0, btab[0], late, rec1)
        with ExitStack() as st:
            xall = sb("x_res", [P, NB, D], F32, st)
            with ExitStack() as s2:
                node_stage(nc, s2, a, c, "attn", 0, xall, regA, acc, ltab, out)
            for l in range(LAYERS):
                with ExitStack() as s2:
                    convolution(nc, s2, c, l, regA, acc, ltab[l], rec1, btab[1])
                with ExitStack() as s2:
                    last = l == LAYERS - 1
                    node_stage(nc, s2, a, c, "last" if last else "mid", l + 1, xall, regA, acc, ltab, out)


def constants(nc, c):
    with ExitStack() as st:
        ii = st.enter_context(nc.sbuf_tensor("ii", [P, P], I32))
        ic = st.enter_context(nc.sbuf_tensor("ic", [P, 1], I32))
        sem = semaphores(nc, st, "i_")
        iota_ready, cast_ready = sem("iota_ready"), sem("cast_ready")
        block = st.enter_context(nc.Block())

        @block.gpsimd
        def _(pool):
            nc.gpsimd.iota(ii[:], [[1, P]], base=0, channel_multiplier=0).then_inc(iota_ready, 1)
            nc.gpsimd.iota(ic[:], [[0, 1]], base=0, channel_multiplier=1).then_inc(iota_ready, 1)

        @block.vector
        def _(dve):
            nc.vector.memset(c["ones"][:], 1.0)
            nc.vector.memset(c["half_pi"][:], HALF_PI)
            nc.vector.memset(c["eps"][:], EPS)
            dve.wait_ge(iota_ready, 2)
            nc.vector.tensor_copy(c["iota"][:], ii[:])
            nc.vector.tensor_copy(c["icol"][:], ic[:]).then_inc(cast_ready, 1)
            dve.wait_ge(cast_ready, 1)
            nc.vector.tensor_scalar(c["ident"][:], c["iota"][:], c["icol"][:, 0:1], None, ALU.is_equal)


def load_nodes(eng, x, dst, sem):
    one = x.shape[1] == 1
    eng.dma_start(dst[:, 0:FULL, :], x[0:FULL * P, :].rearrange("(b p) d -> p b d", p=P),
                  allow_slow_non_contiguous=one).then_inc(sem, 16)
    eng.dma_start(dst[0:REST, FULL, :], x[FULL * P:N, :]).then_inc(sem, 16)


def node_tables(nc, st, a, c, xall, q_all, kvtab, rec0, rec1, acc):
    def sb(name, shape, dt=F32):
        return st.enter_context(nc.sbuf_tensor("n_" + name, shape, dt))

    sem = semaphores(nc, st, "n_")

    w = sb("w", [P, 3, D])
    bias = sb("bias", [P, 3, D])
    nv = sb("nv", [P, NB, 1])
    xs = sb("xs", [P, SB, D])
    xT = sb("xT", [P, SB, D])
    kv = sb("kv", [P, SB, KV])
    fill0 = sb("fill0", [P, GROUP, R0])
    fill1 = sb("fill1", [P, MAX_TILES, R1])
    psT = st.enter_context(nc.psum_tensor("n_psT", [P, 1024], F32))
    ps = [st.enter_context(nc.psum_tensor(f"n_ps{k}", [P, 1024], F32)) for k in range(3)]
    zeroed, loaded, small, filled, stored0 = sem("zeroed"), sem("loaded"), sem("small"), sem("filled"), sem("stored0")
    bias_ready = sem("bias_ready")
    xs_ready, turned, xT_ready, products = sem("xs_ready"), sem("turned"), sem("xT_ready"), sem("products")
    nv_ready, kv_ready, kv_stored, q_ready = sem("nv_ready"), sem("kv_ready"), sem("kv_stored"), sem("q_ready")
    block = st.enter_context(nc.Block())

    @block.sync
    def _(sp):
        sp.wait_ge(zeroed, 1)
        load_nodes(sp, a["x"], xall, loaded)
        load_nodes(sp, a["node_vec"].rearrange("(n o) -> n o", o=1), nv, loaded)
        for k, n in enumerate("qkv"):
            sp.dma_start(w[:, k, :], a[f"L0_gnn_W{n}"]).then_inc(small, 16)
            sp.dma_start(bias[:, k, :], a[f"L0_gnn_b{n}"].rearrange("(o d) -> o d", o=1).broadcast_to([P, D])).then_inc(small, 16)
        kvt = kvtab.rearrange("(b p) d -> p b d", p=P)
        with sp.Fori(0, NSTEP) as i:
            sp.wait_ge(kv_ready, i + 1)
            sp.dma_start(kvt[:, bass.ds(i * SB, SB), :], kv[:]).then_inc(kv_stored, 16)
        sp.wait_ge(kv_stored, 16 * NSTEP)

    @block.gpsimd
    def _(pool):
        nc.gpsimd.memset(xall[:, FULL, :], 0.0)
        nc.gpsimd.memset(nv[:, FULL, :], 0.0).then_inc(zeroed, 1)
        nc.gpsimd.memset(fill0[:], 0.0).then_inc(filled, 1)
        nc.gpsimd.memset(fill1[:], 0.0).then_inc(filled, 1)
        pool.wait_ge(filled, 2)
        nc.gpsimd.memset(fill0[:, :, 2], -1.0).then_inc(filled, 1)
        nc.gpsimd.memset(fill1[:, :, 1], -1.0).then_inc(filled, 1)
        nc.gpsimd.memset(acc[:], 0.0)

    @block.scalar
    def _(act):
        act.wait_ge(filled, 4)
        act.dma_start(rec1.rearrange("(p t) d -> p t d", p=P), fill1[:]).then_inc(stored0, 16)
        r0 = rec0.rearrange("(g p t) d -> p g (t d)", p=P, t=GROUP)
        half = MAX_TILES // GROUP // 4
        for k in range(4):
            act.dma_start(r0[:, k * half:(k + 1) * half, :],
                          fill0[:].rearrange("p t d -> p (t d)").unsqueeze(1).broadcast_to([P, half, GROUP * R0])).then_inc(stored0, 16)
        act.wait_ge(loaded, 64)

        def turn(i):
            wait_used(act, turned, i)
            nc.scalar.copy(xs[:], xall[:, bass.ds(i * SB, SB), :]).then_inc(xs_ready, 1)
            wait_used(act, kv_stored, 16 * i)
            nc.scalar.copy(kv[:, :, 2 * D:KV], nv[:, bass.ds(i * SB, SB), :]).then_inc(nv_ready, 1)

        turns(act, 1, NSTEP, turn)
        act.wait_ge(stored0, 80)

    @block.tensor
    def _(pe):
        pe.wait_ge(small, 96)

        def turn(i):
            pe.wait_ge(xs_ready, i + 1)
            wait_used(pe, xT_ready, i)
            for j in range(SB):
                m = nc.tensor.transpose(psT[:, j * D:(j + 1) * D], xs[:, j, :], c["ident"][:])
            m.then_inc(turned, 1)
            pe.wait_ge(xT_ready, i + 1)
            wait_used(pe, kv_ready, i)
            wait_used(pe, q_ready, i)
            for k in range(3):
                for j in range(SB):
                    m = nc.tensor.matmul(ps[k][:, j * D:(j + 1) * D], xT[:, j, :], w[:, k, :], start=True, stop=True)
            m.then_inc(products, 1)

        turns(pe, 1, NSTEP, turn)

    @block.vector
    def _(dve):
        dve.wait_ge(small, 96)
        nc.vector.tensor_scalar(bias[:, 0, :], bias[:, 0, :], CH ** -0.5, None, ALU.mult).then_inc(bias_ready, 1)
        dve.wait_ge(bias_ready, 1)

        def turn(i):
            dve.wait_ge(turned, i + 1)
            wait_used(dve, products, i)
            nc.vector.tensor_copy(xT[:].rearrange("p b d -> p (b d)"), psT[:, 0:SB * D]).then_inc(xT_ready, 1)
            dve.wait_ge(products, i + 1)

            def view(k):
                return ps[k][:, 0:SB * D].rearrange("p (b d) -> p b d", d=D)

            def bb(k):
                return bias[:, k, :].unsqueeze(1).broadcast_to([P, SB, D])

            nc.vector.scalar_tensor_tensor(q_all[:, bass.ds(i * SB, SB), :], view(0), CH ** -0.5, bb(0),
                                           ALU.mult, ALU.add).then_inc(q_ready, 1)
            wait_used(dve, kv_stored, 16 * i)
            nc.vector.tensor_tensor(kv[:, :, 0:D], view(1), bb(1), ALU.add)
            dve.wait_ge(nv_ready, i + 1)
            nc.vector.tensor_tensor(kv[:, :, D:2 * D], view(2), bb(2), ALU.add).then_inc(kv_ready, 1)

        turns(dve, 1, NSTEP, turn)


def bin_edges(nc, st, a, c, late, rec0, btab):
    def sb(name, shape, dt=F32):
        return st.enter_context(nc.sbuf_tensor("b_" + name, shape, dt))

    sem = semaphores(nc, st, "b_")

    def two(f, name, *more):
        return [f(f"{name}{k}", *more) for k in range(2)]

    keys = two(sb, "keys", [EP, EC], I32)
    times = sb("times", [EP, EC])
    tmp = sb("tmp", [EP, EC], I32)
    bucket = two(sb, "bucket", [EP, EC], BF16)
    place = sb("place", [EP, EC])
    iota_b = sb("iota_b", [EP, NB], BF16)
    before = sb("before", [EP, EP], BF16)
    rest = sb("rest", [EP, EP], BF16)
    ones_b = sb("ones_b", [EP, EP], BF16)
    hot = [two(sb, f"hot{k}_", [EP, STREAMS, NB], BF16) for k in range(2)]
    cnt = two(sb, "cnt", [EP, STREAMS, NB])
    start = two(sb, "start", [EP, STREAMS, NB])
    bins = two(sb, "bins", [EP, 4, NB])
    tiles_i = sb("tiles_i", [EP, NB], I32)
    TP = 111
    tcols = TBL // TP
    tid_i = sb("tid_i", [TP, tcols], I32)
    tid = sb("tid", [TP, tcols])
    ended = sb("ended", [TP, tcols, NB])
    bt = sb("bt", [TP, tcols])
    bt_i = two(sb, "bt_i", [TP, tcols], I32)
    hit = two(sb, "hit", [EP, STREAMS, NB])
    posf = sb("posf", [EP, 2, STREAMS])
    pos = sb("pos", [EP, 2, STREAMS], I32)
    at_place = sb("at_place", [EP, 2, STREAMS], I32)
    at_tile = sb("at_tile", [EP, 2, STREAMS], I32)
    at_group = sb("at_group", [EP, STREAMS], I32)
    in_group = sb("in_group", [EP, STREAMS], I32)
    slot = [sb(f"slot{k}", [EP, STREAMS], I32) for k in range(4)]
    recs = [sb(f"recs{k}", [EP, STREAMS, R0]) for k in range(4)]
    ps_cnt = [st.enter_context(nc.psum_tensor(f"b_ps_cnt{k}", [P, 512], F32)) for k in range(2)]
    ps_pos = [st.enter_context(nc.psum_tensor(f"b_ps_pos{k}", [P, 512], F32)) for k in range(2)]
    assert TP * tcols == TBL

    edges_in, prep, prep_done, fill_done = sem("edges_in"), sem("prep"), sem("prep_done"), sem("fill_done")
    hot_ready, hot_used, start_ready = two(sem, "hot_ready"), two(sem, "hot_used"), sem("start_ready")
    table_ready, table_stored, turn_begun = sem("table_ready"), sem("table_stored"), sem("turn_begun")
    rank_hot_ready, rank_ready, rank_read = two(sem, "rank_hot_ready"), two(sem, "rank_ready"), two(sem, "rank_read")
    pos_step, slot_ready, payload_ready = sem("pos_step"), sem("slot_ready"), sem("payload_ready")
    message_in = [sem(f"message_in{k}") for k in range(4)]
    scattered = [sem(f"scattered{k}") for k in range(4)]
    quarter = STEPS // 4
    block = st.enter_context(nc.Block())

    def cols(t, q):
        return t[:, bass.ds(q * STREAMS, STREAMS)]

    def flat(t):
        return t[:].rearrange("p s b -> p (s b)")

    @block.sync
    def _(sp):
        sp.dma_start(keys[0][:], a["dst"].rearrange("(p c) -> p c", p=EP)).then_inc(edges_in, 16)
        sp.dma_start(keys[1][:], a["src"].rearrange("(p c) -> p c", p=EP)).then_inc(edges_in, 16)
        sp.dma_start(times[:], a["edge_weight"].rearrange("(p c) -> p c", p=EP)).then_inc(edges_in, 16)
        msgs = a["edge_attr_64"].rearrange("(p c) d -> p c d", p=EP)

        def turn(i):
            for u in range(4):
                wait_used(sp, scattered[u], 16 * STREAMS * i)
                sp.dma_start(recs[u][:, :, 4:R0], msgs[:, bass.ds((4 * i + u) * STREAMS, STREAMS), :]).then_inc(message_in[u], 16)

        turns(sp, 1, quarter, turn)
        sp.wait_ge(table_ready, 2)
        for k in range(2):
            sp.dma_start(btab[k].rearrange("(p c) -> p c", p=TP), bt_i[k][:]).then_inc(table_stored, 16)
        sp.wait_ge(table_stored, 32)

    @block.gpsimd
    def _(pool):
        nc.gpsimd.iota(tid_i[:], [[1, tcols]], base=0, channel_multiplier=tcols)
        for k in range(4):
            m = nc.gpsimd.memset(recs[k][:, :, 3], 0.0)
        m.then_inc(fill_done, 1)
        pool.wait_ge(fill_done, 1)
        with pool.Fori(0, quarter) as i:
            for u in range(4):
                pool.wait_ge(slot_ready, 4 * i + (u + 1))
                pool.wait_ge(payload_ready, 4 * i + (u + 1))
                pool.wait_ge(message_in[u], 16 * i + 16)
                pool.sem_inc(turn_begun, 1)
                for j in range(STREAMS):
                    nc.gpsimd.indirect_dma_start(
                        out=rec0, out_offset=bass.IndirectOffsetOnAxis(slot[u][:, j:j + 1].bitcast(U32), 0),
                        in_=recs[u][:, j, :], in_offset=None).then_inc(scattered[u], 16)
        for u in range(4):
            pool.wait_ge(scattered[u], 16 * STREAMS * quarter)

    @block.scalar
    def _(act):
        act.wait_ge(edges_in, 48)
        act.wait_ge(prep_done, 1)

        def turn(i):
            for u in range(4):
                wait_used(act, scattered[u], 16 * STREAMS * i)
                q = 4 * i + u
                nc.scalar.copy(recs[u][:, :, 0], cols(times, q))
                nc.scalar.copy(recs[u][:].bitcast(I32)[:, :, 1], cols(keys[1], q))
                nc.scalar.copy(recs[u][:, :, 2], cols(place, q)).then_inc(payload_ready, 1)

        turns(act, 1, quarter, turn)

    @block.tensor
    def _(pe):
        pe.wait_ge(prep_done, 1)
        for k in range(2):
            nc.tensor.matmul(ps_cnt[k][0:EP, 0:BINS], ones_b[:], flat(hot[k][1]), start=True, stop=True).then_inc(hot_used[k], 1)
        with pe.Fori(0, quarter) as i:
            for u in range(4):
                for k in range(2):
                    pe.wait_ge(hot_ready[k], 4 * i + (u + 1))
                    nc.tensor.matmul(ps_cnt[k][0:EP, 0:BINS], ones_b[:], flat(hot[k][u % 2]),
                                     start=False, stop=True, skip_group_check=True).then_inc(hot_used[k], 1)
        pe.wait_ge(start_ready, 1)
        for k in range(2):
            nc.tensor.matmul(ps_pos[k][0:EP, 0:BINS], c["ones"][0:1, 0:EP], start[k][0:1, :, :].rearrange("p s b -> p (s b)"), start=True, stop=True)
        with pe.Fori(0, quarter) as i:
            for u in range(4):
                for k in range(2):
                    pe.wait_ge(rank_hot_ready[k], 4 * i + (u + 1))
                    nc.tensor.matmul(ps_pos[k][0:EP, 0:BINS], before[:], flat(hot[k][u % 2]), start=False, stop=True,
                                     skip_group_check=True).then_inc(rank_ready[k], 1)
                for k in range(2):
                    pe.wait_ge(rank_read[k], 4 * i + (u + 1))
                    nc.tensor.matmul(ps_pos[k][0:EP, 0:BINS], rest[:], flat(hot[k][u % 2]), start=False, stop=True, skip_group_check=True)

    @block.vector
    def _(dve):
        dve.wait_ge(edges_in, 48)
        ch = Chain(dve, prep, 0)
        nc.vector.tensor_copy(late[:, :, 0], keys[0][:])
        for k in range(2):
            ch.then(nc.vector.tensor_scalar(tmp[:], keys[k][:], 7, None, ALU.logical_shift_right))
            ch.then(nc.vector.tensor_copy(bucket[k][:], tmp[:]))
            ch.then(nc.vector.tensor_scalar(tmp[:], keys[k][:], P - 1, None, ALU.bitwise_and))
            ch.then(nc.vector.tensor_copy(place[:] if k == 0 else late[:].bitcast(F32)[:, :, 1], tmp[:]))
        nc.vector.tensor_copy(iota_b[:], c["iota"][0:EP, 0:NB])
        nc.vector.tensor_scalar(before[:], c["iota"][0:EP, 0:EP], c["icol"][0:EP, 0:1], None, ALU.is_gt)
        nc.vector.tensor_scalar(rest[:], c["iota"][0:EP, 0:EP], c["icol"][0:EP, 0:1], None, ALU.is_le)
        nc.vector.memset(ones_b[:], 1.0)
        nc.vector.memset(hot[0][1][:], 0.0)
        ch.then(nc.vector.memset(hot[1][1][:], 0.0))
        dve.sem_inc(prep_done, 1)

        def one_hot(k, u, q):
            return nc.vector.tensor_tensor(
                hot[k][u % 2][:], cols(bucket[k], q).unsqueeze(2).broadcast_to([EP, STREAMS, NB]),
                iota_b[:].unsqueeze(1).broadcast_to([EP, STREAMS, NB]), ALU.is_equal)

        def count(i):
            for u in range(4):
                for k in range(2):
                    wait_used(dve, hot_used[k], 4 * i + u)
                    one_hot(k, u, 4 * i + u).then_inc(hot_ready[k], 1)

        turns(dve, 1, quarter, count)
        dve.wait_ge(fill_done, 1)
        ch.then(nc.vector.tensor_copy(tid[:], tid_i[:]))
        for k in range(2):
            b_ = bins[k]
            dve.wait_ge(hot_used[k], STEPS + 1)
            ch.then(nc.vector.tensor_copy(flat(cnt[k]), ps_cnt[k][0:EP, 0:BINS]))
            ch.then(nc.vector.tensor_reduce(b_[:, 0, :], cnt[k][:].rearrange("p s b -> p b s"), AX.X, ALU.add))
            ch.then(nc.vector.tensor_scalar(b_[:, 1, :], b_[:, 0, :], float(P - 1), None, ALU.add))
            ch.then(nc.vector.tensor_copy(tiles_i[:], b_[:, 1, :]))
            ch.then(nc.vector.tensor_scalar(tiles_i[:], tiles_i[:], 7, None, ALU.logical_shift_right))
            ch.then(nc.vector.tensor_copy(b_[:, 1, :], tiles_i[:]))
            ch.then(nc.vector.memset(b_[:, 3, :], 0.0))
            ch.then(nc.vector.tensor_tensor_scan(b_[:, 2, :], b_[:, 1, :], b_[:, 3, :], 0.0, ALU.add, ALU.add))
            ch.then(nc.vector.tensor_tensor(b_[:, 3, :], b_[:, 2, :], b_[:, 1, :], ALU.subtract))
            ch.then(nc.vector.tensor_scalar(start[k][:, 0, :], b_[:, 3, :], float(P), None, ALU.mult))
            for s in range(1, STREAMS):
                ch.then(nc.vector.tensor_tensor(start[k][:, s, :], start[k][:, s - 1, :], cnt[k][:, s - 1, :], ALU.add))
        dve.sem_inc(start_ready, 1)

        def rank(i):
            for u in range(4):
                q = 4 * i + u
                cs = Chain(dve, pos_step, 28 * i + 7 * u)
                for k in range(2):
                    one_hot(k, u, q).then_inc(rank_hot_ready[k], 1)
                for k in range(2):
                    dve.wait_ge(rank_hot_ready[k], q + 1)
                    dve.wait_ge(rank_ready[k], q + 1)
                    nc.vector.tensor_tensor(flat(hit[k]), flat(hot[k][u % 2]), ps_pos[k][0:EP, 0:BINS], ALU.mult).then_inc(rank_read[k], 1)
                for k in range(2):
                    dve.wait_ge(rank_read[k], q + 1)
                    m = nc.vector.tensor_reduce(posf[:, k, :], hit[k][:], AX.X, ALU.add)
                    if k == 0:
                        m.then_inc(pos_step, 1)
                        cs.n += 1
                cs.then(m)
                cs.then(nc.vector.tensor_copy(pos[:], posf[:]))
                nc.vector.tensor_scalar(at_place[:], pos[:], P - 1, None, ALU.bitwise_and).then_inc(pos_step, 1)
                cs.n += 1
                cs.then(nc.vector.tensor_scalar(at_tile[:], pos[:], 7, None, ALU.logical_shift_right))
                nc.vector.scalar_tensor_tensor(cols(late, q)[:, :, 2], at_place[:, 1, :], float(MAX_TILES), at_tile[:, 1, :], ALU.mult, ALU.add)
                nc.vector.scalar_tensor_tensor(in_group[:], at_place[:, 0, :], float(GROUP), at_tile[:, 0, :], ALU.mult, ALU.add).then_inc(pos_step, 1)
                cs.n += 1
                cs.then(nc.vector.tensor_scalar(at_group[:], at_tile[:, 0, :], 3, None, ALU.logical_shift_right))
                wait_used(dve, scattered[u], 16 * STREAMS * i)
                nc.vector.scalar_tensor_tensor(slot[u][:], at_group[:], float(P * GROUP - GROUP), in_group[:],
                                               ALU.mult, ALU.add).then_inc(slot_ready, 1)
                assert cs.n == 7

        turns(dve, 1, quarter, rank)
        for k in range(2):
            ch.then(nc.vector.tensor_tensor(ended[:], bins[k][0:TP, 2, :].unsqueeze(1).broadcast_to([TP, tcols, NB]),
                                            tid[:].unsqueeze(2).broadcast_to([TP, tcols, NB]), ALU.is_le))
            ch.then(nc.vector.tensor_reduce(bt[:], ended[:], AX.X, ALU.add))
            nc.vector.tensor_scalar(bt_i[k][:], bt[:], float(NB - 1), None, ALU.min).then_inc(table_ready, 1)
            dve.wait_ge(table_ready, k + 1)


def attention(nc, st, a, c, q_all, acc, kvtab, rec0, btab, late, rec1):
    def sb(name, shape, dt=F32):
        return st.enter_context(nc.sbuf_tensor("a_" + name, shape, dt))

    sem = semaphores(nc, st, "a_")

    def ps(name, width=512):
        return st.enter_context(nc.psum_tensor("a_" + name, [P, width], F32))

    LATE = EC // 4
    assert 4 * LATE == EC and LATE <= QUADS
    out_rec = [sb(f"out_rec{k}", [EP, 4, 3], I32) for k in range(4)]
    out_ready = sem("out_ready")
    scattered = [sem(f"scattered{k}") for k in range(4)]
    we = sb("we", [MSG + TDIM, D])
    tw = sb("tw", [P, TDIM])
    tb = sb("tb", [P, TDIM])
    brow = sb("brow", [1, TBL], I32)
    ball = sb("ball", [P, TBL], I32)
    pen = sb("pen", [P, TBL])
    rec = [sb(f"rec{k}", [P, GROUP, R0E]) for k in range(2)]
    g = [sb(f"g{k}", [P, 4, KV]) for k in range(4)]
    hot = [sb(f"hot{k}", [P, 4, P]) for k in range(4)]
    miss = [sb(f"miss{k}", [P, 4, P]) for k in range(2)]
    hotT = [sb(f"hotT{k}", [P, 4 * P]) for k in range(4)]
    eaT = [sb(f"eaT{k}", [MSG + TDIM, 4 * P]) for k in range(2)]
    rel = sb("rel", [P, GROUP])
    arg = sb("arg", [P, GROUP, TDIM])
    cyc = sb("cyc", [P, GROUP, TDIM])
    zz = sb("zz", [P, GROUP, TDIM])
    kk = sb("kk", [P, 4, D])
    vv = [sb(f"vv{k}", [P, 4, D]) for k in range(2)]
    score = [sb(f"score{k}", [P, 4, HEADS]) for k in range(2)]
    sc = sb("sc", [P, 4, HEADS, P])
    tmax = sb("tmax", [P, 4, HEADS])
    mx = [sb(f"mx{k}", [P, 5, HEADS]) for k in range(2)]
    old = sb("old", [P, 4, HEADS])
    penq = [sb(f"penq{k}", [P, 4]) for k in range(4)]
    dd = [sb(f"dd{k}", [P, 2, 4, HEADS]) for k in range(2)]
    ex = [sb(f"ex{k}", [P, 2, 4, HEADS]) for k in range(2)]
    wv = [sb(f"wv{k}", [P, 4, HEADS, HW]) for k in range(2)]
    psT, psE, psM, psQ = ps("psT"), ps("psE"), ps("psM"), ps("psQ")
    psX, psA = ps("psX", 1024), ps("psA", 1024)

    small, table_in, pen_step, pen_ready, turn_begun = sem("small"), sem("table_in"), sem("pen_step"), sem("pen_ready"), sem("turn_begun")
    rec_in = [sem(f"rec_in{k}") for k in range(2)]
    gathered = [sem(f"gathered{k}") for k in range(4)]
    miss_ready, hot_ready, angle_ready, enc_ready = sem("miss_ready"), sem("hot_ready"), sem("angle_ready"), sem("enc_ready")
    ea_turned, eaT_ready, hot_turned, hotT_ready = sem("ea_turned"), sem("eaT_ready"), sem("hot_turned"), sem("hotT_ready")
    e_ready, qg_ready, vv_ready, qk_ready, sc_ready = sem("e_ready"), sem("qg_ready"), sem("vv_ready"), sem("qk_ready"), sem("sc_ready")
    sc_turned, tmax_ready, mx_ready, m_ready, dd_ready = sem("sc_turned"), sem("tmax_ready"), sem("mx_ready"), sem("m_ready"), sem("dd_ready")
    kk_ready, ex_ready, wv_ready, sum_ready, added, pen_in = sem("kk_ready"), sem("ex_ready"), sem("wv_ready"), sem("sum_ready"), sem("added"), sem("pen_in")
    enc_step, abs_ready, score_ready, mx_step = sem("enc_step"), sem("abs_ready"), sem("score_ready"), sem("mx_step")
    block = st.enter_context(nc.Block())

    def sums(i):
        at = 512 * (i // 2) + (i % 2) * HEADS * HW
        return psA[:, at:at + HEADS * HW]

    groups = QUADS // 2
    TOTAL = QUADS + 2

    def steps(eng, body):
        fours = (QUADS - 2) // 4
        for q in range(2):
            body(q, q % 4, (q // 2 + 1) if q % 2 == 0 else None)
        with eng.Fori(0, fours) as i:
            for r in range(4):
                body(4 * i + (2 + r), (2 + r) % 4, (2 * i + (2 + r // 2)) if r % 2 == 0 else None)
        for q in range(2 + 4 * fours, TOTAL):
            f = q // 2 + 1
            body(q, q % 4, f if q % 2 == 0 and f < groups else None)

    def live(q):
        return is_loop(q) or 0 <= q < QUADS

    @block.sync
    def _(sp):
        sp.dma_start(we[0:MSG, :], a["L0_gnn_We"][TDIM:TDIM + MSG, :]).then_inc(small, 16)
        sp.dma_start(we[MSG:MSG + TDIM, :], a["L0_gnn_We"][0:TDIM, :]).then_inc(small, 16)
        sp.dma_start(tw[:], a["L0_gnn_time_w"].rearrange("(o d) -> o d", o=1).broadcast_to([P, TDIM])).then_inc(small, 16)
        sp.dma_start(tb[:], a["L0_gnn_time_b"].rearrange("(o d) -> o d", o=1).broadcast_to([P, TDIM])).then_inc(small, 16)
        sp.dma_start(brow[:], btab.rearrange("(o d) -> o d", o=1)).then_inc(table_in, 16)
        sp.dma_start(ball[:], btab.rearrange("(o d) -> o d", o=1).broadcast_to([P, TBL])).then_inc(table_in, 16)
        r0 = rec0.rearrange("(g p t) d -> g p t d", p=P, t=GROUP)

        def load(f, s):
            sp.dma_start(rec[s][:, :, 0:R0], r0[bass.ds(f, 1), :, :, :].rearrange("o p t d -> (o p) t d")).then_inc(rec_in[s], 16)

        load(0, 0)
        load(1, 1)

        def reload(f, s):
            sp.wait_ge(ea_turned, 2 * f - 2)
            sp.wait_ge(hot_ready, 2 * f - 2)
            load(f, s)

        with sp.Fori(0, (groups - 2) // 2) as i:
            reload(2 * i + 2, 0)
            reload(2 * i + 3, 1)

    @block.gpsimd
    def _(pool):
        def front(f, s, k, loop):
            pool.wait_ge(rec_in[s], 16 * k + 16)
            for h in range(2):
                r = 2 * s + h
                if loop:
                    pool.wait_ge(vv_ready, 2 * f + (h - 3))
                pool.sem_inc(turn_begun, 1)
                for j in range(4):
                    idx = rec[s][:, 4 * h + j, 1:2].bitcast(U32)
                    nc.gpsimd.indirect_dma_start(out=g[r][:, j, :], out_offset=None, in_=kvtab,
                                                 in_offset=bass.IndirectOffsetOnAxis(idx, 0)).then_inc(gathered[r], 16)

        def scatter(q, r):
            pool.wait_ge(out_ready, q + 1)
            pool.sem_inc(turn_begun, 1)
            for j in range(4):
                nc.gpsimd.indirect_dma_start(
                    out=rec1, out_offset=bass.IndirectOffsetOnAxis(out_rec[r][:, j, 2:3].bitcast(U32), 0),
                    in_=out_rec[r][:, j, 0:2].bitcast(F32), in_offset=None).then_inc(scattered[r], 16)

        turns_both = (LATE - 2) // 4
        for f in range(2):
            front(f, f, 0, False)
        for r in range(2):
            scatter(r, r)
        with pool.Fori(1, turns_both + 1) as i:
            for s in range(2):
                front(2 * i + s, s, i, True)
                scatter(4 * i + (2 * s - 2), (2 * s - 2) % 4)
                scatter(4 * i + (2 * s - 1), (2 * s - 1) % 4)
        for q in range(4 * turns_both + 2, LATE):
            scatter(q, q % 4)
        with pool.Fori(turns_both + 1, groups // 2) as i:
            for s in range(2):
                front(2 * i + s, s, i, True)
        for r in range(4):
            pool.wait_ge(scattered[r], 64 * ((LATE - r + 3) // 4))

    @block.scalar
    def _(act):
        def encode(f, s):
            act.wait_ge(angle_ready, f + 1)
            nc.scalar.activation(rec[s][:, :, R0:R0E], zz[:], ACT.Abs).then_inc(abs_ready, 1)
            act.wait_ge(abs_ready, f + 1)
            nc.scalar.activation(rec[s][:, :, R0:R0E], rec[s][:, :, R0:R0E], ACT.Sin, bias=c["half_pi"][:, 0:1], scale=-1.0).then_inc(enc_ready, 1)

        def turned_attributes(q, r):
            act.wait_ge(ea_turned, q + 1)
            wait_used(act, e_ready, q - 1)
            nc.scalar.copy(eaT[r % 2][:], psT[0:MSG + TDIM, :]).then_inc(eaT_ready, 1)

        def turned_hot(q, r):
            act.wait_ge(hot_turned, q + 1)
            nc.scalar.copy(hotT[r][:], psT[:]).then_inc(hotT_ready, 1)
            wait_used(act, sc_ready, q - 1)
            nc.scalar.activation(miss[r % 2][:], hot[r][:], ACT.Copy, bias=NEG, scale=-NEG).then_inc(miss_ready, 1)

        def masked(q, r):
            act.wait_ge(score_ready, q + 1)
            act.wait_ge(miss_ready, q + 1)
            wait_used(act, sc_turned, q)
            for j in range(4):
                for h in range(HEADS):
                    m = nc.scalar.activation(sc[:, j, h, :], miss[r % 2][:, j, :], ACT.Identity, bias=score[r % 2][:, j, h:h + 1], scale=1.0)
            m.then_inc(sc_ready, 1)

        def body(q, r, f, k):
            if live(q):
                masked(q, r)
            if live(q - 1):
                wait_used(act, dd_ready, q)
                nc.scalar.activation(ex[(r - 1) % 2][:], dd[(r - 1) % 2][:], ACT.Exp).then_inc(ex_ready, 1)
            if live(q + 2):
                turned_hot(q + 2, (r + 2) % 4)
            if f is not None:
                encode(f, (r // 2 + 1) % 2)
            if live(q + 2):
                turned_attributes(q + 2, (r + 2) % 4)
            if k is not None:
                act.wait_ge(scattered[(r + 3) % 4], 64 * k)
                take(q + 3, (r + 3) % 4)

        def take(q, r):
            nc.scalar.copy(out_rec[r][:], late[:, bass.ds(4 * q, 4), :]).then_inc(out_ready, 1)

        for q in range(4):
            take(q, q)
        encode(0, 0)
        for q in range(2):
            turned_hot(q, q)
            turned_attributes(q, q)
        first = (LATE - 5) // 4
        assert 4 * first + 5 == LATE
        body(0, 0, 1, None)
        body(1, 1, None, 1)
        with act.Fori(0, first) as i:
            for r in range(4):
                body(4 * i + (2 + r), (2 + r) % 4, 2 * i + (2 + r // 2) if r % 2 == 0 else None, i + (5 + r) // 4)
        with act.Fori(first, (QUADS - 2) // 4) as i:
            for r in range(4):
                body(4 * i + (2 + r), (2 + r) % 4, 2 * i + (2 + r // 2) if r % 2 == 0 else None, None)
        for q in range(2 + 4 * ((QUADS - 2) // 4), TOTAL):
            body(q, q % 4, q // 2 + 1 if q % 2 == 0 and q // 2 + 1 < groups else None, None)

    @block.tensor
    def _(pe):
        def turn_hot(q, r):
            pe.wait_ge(hot_ready, q + 1)
            wait_used(pe, eaT_ready, q)
            for j in range(4):
                m = nc.tensor.transpose(psT[:, j * P:(j + 1) * P], hot[r][:, j, :], c["ident"][:])
            m.then_inc(hot_turned, 1)

        def turn_attributes(q, r, f):
            if f is not None:
                pe.wait_ge(enc_ready, f + 1)
            pe.wait_ge(hotT_ready, q + 1)
            for j in range(4):
                m = nc.tensor.transpose(psT[0:MSG + TDIM, j * P:(j + 1) * P], rec[r // 2][:, 4 * (r % 2) + j, 4:R0E], c["ident"][:])
            m.then_inc(ea_turned, 1)

        def edge(q, r):
            pe.wait_ge(eaT_ready, q + 1)
            wait_used(pe, vv_ready, q)
            for j in range(4):
                m = nc.tensor.matmul(psE[:, j * D:(j + 1) * D], eaT[r % 2][:, j * P:(j + 1) * P], we[:], start=True, stop=True)
            m.then_inc(e_ready, 1)

        def query(q, r):
            pe.wait_ge(hotT_ready, q + 1)
            wait_used(pe, qk_ready, q)
            _, bs = nc.values_load_multi_w_load_instructions(brow[0:1, bass.ds(4 * q, 4)], engines=[mybir.EngineType.PE],
                                                             min_val=0, max_val=NB - 1, skip_runtime_bounds_check_because="the table is clamped to the last bucket")
            for j in range(4):
                m = nc.tensor.matmul(psQ[:, j * D:(j + 1) * D], hotT[r][:, j * P:(j + 1) * P], q_all[:, bass.ds(bs[j], 1), :].rearrange("p o d -> p (o d)"),
                                     start=True, stop=True)
            m.then_inc(qg_ready, 1)

        def body(q, r, f):
            p = (r - 1) % 4
            if live(q - 1):
                wait_used(pe, mx_ready, q)
                for j in range(4):
                    m = nc.tensor.matmul(psM[:, 2 * j:2 * j + 2], hotT[p][:, j * P:(j + 1) * P], mx[p % 2][:, j + 1, :], start=True, stop=True)
                m.then_inc(m_ready, 1)
            if live(q + 1):
                edge(q + 1, (r + 1) % 4)
                query(q + 1, (r + 1) % 4)
            if live(q):
                pe.wait_ge(sc_ready, q + 1)
                wait_used(pe, tmax_ready, q)
                for j in range(4):
                    for h in range(HEADS):
                        m = nc.tensor.transpose(psX[:, (2 * j + h) * P:(2 * j + h + 1) * P], sc[:, j, h, :], c["ident"][:])
                m.then_inc(sc_turned, 1)
            if live(q + 2):
                turn_hot(q + 2, (r + 2) % 4)
            if live(q - 1):
                wait_used(pe, wv_ready, q)
                for j in range(4):
                    m = nc.tensor.matmul(sums(j), hot[p][:, j, :], wv[p % 2][:, j, :, :].rearrange("p h w -> p (h w)"), start=True, stop=True)
                m.then_inc(sum_ready, 1)
            if live(q + 2):
                turn_attributes(q + 2, (r + 2) % 4, f)

        pe.wait_ge(small, 64)
        pe.wait_ge(table_in, 32)
        for q in range(2):
            turn_hot(q, q)
            turn_attributes(q, q, 0 if q == 0 else None)
        edge(0, 0)
        query(0, 0)
        steps(pe, body)

    @block.vector
    def _(dve):
        def front(f, s, k, q):
            for h in range(2):
                r = 2 * s + h
                dve.wait_ge(gathered[r], 64 * k + 64)
                m = nc.vector.tensor_tensor(rel[:, 4 * h:4 * h + 4], g[r][:, :, 2 * D], rec[s][:, 4 * h:4 * h + 4, 0], ALU.subtract)
            cs = Chain(dve, enc_step, 6 * f)
            cs.then(m)
            tw_b = tw[:].unsqueeze(1).broadcast_to([P, GROUP, TDIM])
            cs.then(nc.vector.tensor_tensor(arg[:], rel[:].unsqueeze(2).broadcast_to([P, GROUP, TDIM]), tw_b, ALU.mult))
            cs.then(nc.vector.tensor_tensor(arg[:], arg[:], tb[:].unsqueeze(1).broadcast_to([P, GROUP, TDIM]), ALU.add))
            cs.then(nc.vector.tensor_scalar(cyc[:], arg[:], INV_TWO_PI, MAGIC, ALU.mult, ALU.add))
            cs.then(nc.vector.tensor_scalar(cyc[:], cyc[:], MAGIC, None, ALU.subtract))
            cs.then(nc.vector.scalar_tensor_tensor(arg[:], cyc[:], -TWO_PI_HI, arg[:], ALU.mult, ALU.add))
            wait_used(dve, enc_ready, f)
            nc.vector.scalar_tensor_tensor(zz[:], cyc[:], -TWO_PI_LO, arg[:], ALU.mult, ALU.add).then_inc(angle_ready, 1)

        def one_hot(q, r):
            if is_loop(q) or q >= 4:
                dve.wait_ge(sum_ready, q - 3)
            h = r % 2
            nc.vector.tensor_tensor(hot[r][:], rec[r // 2][:, 4 * h:4 * h + 4, 2:3].broadcast_to([P, 4, P]),
                                    c["iota"][:].unsqueeze(1).broadcast_to([P, 4, P]), ALU.is_equal).then_inc(hot_ready, 1)

        def scores(q, r):
            e4 = psE[:].rearrange("p (t d) -> p t d", d=D)
            dve.wait_ge(e_ready, q + 1)
            wait_used(dve, score_ready, q)
            nc.vector.tensor_tensor(kk[:], e4, g[r][:, :, 0:D], ALU.add).then_inc(kk_ready, 1)
            if is_loop(q) or q >= 2:
                dve.wait_ge(wv_ready, q - 1)
            nc.vector.tensor_tensor(vv[r % 2][:], e4, g[r][:, :, D:2 * D], ALU.add).then_inc(vv_ready, 1)
            dve.wait_ge(kk_ready, q + 1)
            dve.wait_ge(qg_ready, q + 1)
            nc.vector.tensor_tensor(kk[:], kk[:], psQ[:].rearrange("p (t d) -> p t d", d=D), ALU.mult).then_inc(qk_ready, 1)

        def summed_scores(q, r):
            dve.wait_ge(qk_ready, q + 1)
            nc.vector.tensor_reduce(score[r % 2][:].rearrange("p t h -> p (t h)"), kk[:].rearrange("p t (h d) -> p (t h) d", h=HEADS),
                                    AX.X, ALU.add).then_inc(score_ready, 1)

        def penalties(q, r):
            nc.vector.tensor_copy(penq[r][:], pen[:, bass.ds(4 * q, 4)]).then_inc(mx_step, 1)
            nc.vector.tensor_copy(mx[r % 2][:, 0, :], mx[(r + 1) % 2][:, 4, :]).then_inc(mx_step, 1)

        def maxima(q, r):
            m_ = mx[r % 2]
            dve.wait_ge(mx_step, 6 * q + 2)
            dve.wait_ge(sc_turned, q + 1)
            nc.vector.tensor_reduce(tmax[:].rearrange("p t h -> p (t h)"), psX[:].rearrange("p (t d) -> p t d", d=P), AX.X, ALU.max).then_inc(tmax_ready, 1)
            dve.wait_ge(tmax_ready, q + 1)
            for h in range(HEADS):
                m = nc.vector.tensor_tensor_scan(m_[:, 1:5, h], penq[r][:], tmax[:, :, h], m_[:, 0, h:h + 1], ALU.add, ALU.max)
            m.then_inc(mx_ready, 1)

        def exponents(q, r, step):
            m_, d = mx[r % 2], dd[r % 2]
            if step == 0:
                dve.wait_ge(mx_ready, q + 1)
                nc.vector.tensor_tensor(old[:], m_[:, 0:4, :], penq[r][:].unsqueeze(2).broadcast_to([P, 4, HEADS]), ALU.add).then_inc(mx_step, 1)
            elif step == 1:
                dve.wait_ge(m_ready, q + 1)
                nc.vector.tensor_tensor(d[:, 0, :, :].rearrange("p t h -> p (t h)"), score[r % 2][:].rearrange("p t h -> p (t h)"),
                                        psM[:, 0:8], ALU.subtract).then_inc(mx_step, 1)
            elif step == 2:
                dve.wait_ge(mx_step, 6 * q + 3)
                nc.vector.tensor_tensor(d[:, 1, :, :], old[:], m_[:, 1:5, :], ALU.subtract).then_inc(mx_step, 1)
            elif step == 3:
                dve.wait_ge(mx_step, 6 * q + 4)
                nc.vector.tensor_scalar(d[:, 0, :, :], d[:, 0, :, :], 0.0, None, ALU.min).then_inc(mx_step, 1)
            else:
                dve.wait_ge(mx_step, 6 * q + 6)
                dve.sem_inc(dd_ready, 1)

        def weigh(q, r):
            dve.wait_ge(ex_ready, q + 1)
            e = ex[r % 2][:, 0, :, :]
            nc.vector.tensor_tensor(wv[r % 2][:, :, :, 0:CH], vv[r % 2][:].rearrange("p t (h d) -> p t h d", h=HEADS),
                                    e.unsqueeze(3).broadcast_to([P, 4, HEADS, CH]), ALU.mult)
            nc.vector.tensor_copy(wv[r % 2][:, :, :, CH], e).then_inc(wv_ready, 1)

        def buckets(q):
            dve.wait_ge(table_in, 32)
            _, bs = nc.values_load_multi_w_load_instructions(brow[0:1, bass.ds(4 * q, 4)], engines=[mybir.EngineType.DVE],
                                                             min_val=0, max_val=NB - 1, skip_runtime_bounds_check_because="the table is clamped to the last bucket")
            return bs

        def add(q, r, bs, n):
            j, h = n // HEADS, n % HEADS
            dve.wait_ge(added, 8 * q + max(n, 1))
            at = acc[:, bass.ds(bs[j], 1), h * HW:(h + 1) * HW].rearrange("p o w -> p (o w)")
            nc.vector.scalar_tensor_tensor(at, at, ex[r % 2][:, 1, j, h:h + 1], sums(j)[:, h * HW:(h + 1) * HW],
                                           ALU.mult, ALU.add).then_inc(added, 1)

        def body(q, r, f):
            if live(q):
                scores(q, r)
            if live(q - 1):
                penalties(q - 1, (r - 1) % 4)
            if live(q):
                summed_scores(q, r)
            if live(q - 1):
                maxima(q - 1, (r - 1) % 4)
            if live(q - 2):
                bs = buckets(q - 2)
                dve.wait_ge(sum_ready, q - 1)
            for n in range(8):
                if live(q - 2):
                    add(q - 2, (r - 2) % 4, bs, n)
                if live(q - 1) and n >= 5:
                    exponents(q - 1, (r - 1) % 4, n - 5)
            if live(q - 1):
                exponents(q - 1, (r - 1) % 4, 3)
                exponents(q - 1, (r - 1) % 4, 4)
            if f is not None:
                s = (r // 2 + 1) % 2
                k = f // 2 if isinstance(f, int) else (f - s) // 2
                dve.wait_ge(rec_in[s], 16 * k + 16)
            if live(q + 2):
                one_hot(q + 2, (r + 2) % 4)
            if f is not None:
                front(f, s, k, q)
            if live(q - 1):
                weigh(q - 1, (r - 1) % 4)

        dve.wait_ge(small, 64)
        dve.wait_ge(table_in, 32)
        cp = Chain(dve, pen_step, 0)
        nc.vector.memset(mx[1][:], NEG)
        cp.then(nc.vector.tensor_copy(pen[:], ball[:]))
        cp.then(nc.vector.tensor_tensor(pen[:, 1:TBL], ball[:, 1:TBL], ball[:, 0:TBL - 1], ALU.not_equal))
        cp.then(nc.vector.memset(pen[:, 0:1], 1.0))
        cp.then(nc.vector.tensor_scalar(pen[:], pen[:], NEG, None, ALU.mult))
        dve.sem_inc(pen_ready, 1)
        dve.sem_inc(added, 1)
        front(0, 0, 0, 0)
        one_hot(0, 0)
        one_hot(1, 1)
        steps(dve, body)


def node_stage(nc, st, a, c, kind, layer, xall, s1_all, acc, ltab, out):
    pre = f"s{layer}_"

    def sb(name, shape, dt=F32):
        return st.enter_context(nc.sbuf_tensor(pre + name, shape, dt))

    sem = semaphores(nc, st, pre)

    prepare = kind != "last"
    W = [P, SB, D]
    r_, h_ = sb("r", W), sb("h", W)
    sq = sb("sq", W)
    st_ = sb("stats", [P, 4, SB])
    biases = sb("biases", [P, 6, D])
    if kind == "attn":
        xs, wskip, den = sb("xs", W), sb("wskip", [P, D]), sb("den", [P, 2, SB, HEADS])
        bneed = [("L0_gnn_bskip", None)]
    else:
        bneed = [("L1_gnn_gcn_b", layer - 1)]
    if prepare:
        w = sb("w", [P, 3, D])
        hT, dg, trow, s1 = sb("hT", W), sb("dg", W), sb("trow", [P, SB, LR]), sb("s1", [P, 2, SB])
        attb = sb("attb", [P, 1])
        zeros = sb("zeros", [P, SB, HEADS * HW])
    psT = st.enter_context(nc.psum_tensor(pre + "psT", [P, 1024], F32))
    ps = [st.enter_context(nc.psum_tensor(pre + f"ps{k}", [P, 1024], F32)) for k in range(3)]

    def view(t):
        return t[:, 0:SB * D].rearrange("p (b d) -> p b d", d=D)

    def row(k):
        return biases[:, k, :].unsqueeze(1).broadcast_to(W)

    small, xin, x_copied, x_turned, skip_ready = sem("small"), sem("xin"), sem("x_copied"), sem("x_turned"), sem("skip_ready")
    step, var_ready, sd_ready, h_ready, h_turned = sem("step"), sem("var_ready"), sem("sd_ready"), sem("h_ready"), sem("h_turned")
    xT_ready, hT_ready, products, s1_ready, dg_ready = sem("xT_ready"), sem("hT_ready"), sem("products"), sem("s1_ready"), sem("dg_ready")
    spread, spread_read, support_ready, stored, s2_ready = sem("spread"), sem("spread_read"), sem("support_ready"), sem("stored"), sem("s2_ready")
    zeroed, tail_zeroed = sem("zeroed"), sem("tail_zeroed")
    block = st.enter_context(nc.Block())
    nsmall = 0

    @block.sync
    def _(sp):
        def vec(dst, src):
            sp.dma_start(dst, src.broadcast_to(list(dst.shape))).then_inc(small, 16)

        if kind == "attn":
            sp.wait_ge(tail_zeroed, 1)
            load_nodes(sp, a["x"], xall, xin)
            vec(biases[:, 0, :], a["L0_gnn_bskip"].rearrange("(o d) -> o d", o=1))
            sp.dma_start(wskip[:], a["L0_gnn_Wskip"]).then_inc(small, 16)
        else:
            vec(biases[:, 0, :], a["L1_gnn_gcn_b"][layer - 1:layer, :])
            vec(biases[:, 5, :], a["L1_gnn_gcn_b"][layer - 1:layer, :])
        if prepare:
            for k, n in enumerate(("nb", "self", "gcn")):
                sp.dma_start(w[:, k, :], a[f"L1_gnn_{n}_w"][layer]).then_inc(small, 16)
            vec(biases[:, 1, :], a["L1_gnn_nb_b"][layer:layer + 1, :])
            vec(biases[:, 2, :], a["L1_gnn_self_b"][layer:layer + 1, :])
            vec(biases[:, 3, :], a["L1_gnn_att_w"][layer, 0:D, :].rearrange("d o -> o d"))
            vec(biases[:, 4, :], a["L1_gnn_att_w"][layer, D:2 * D, :].rearrange("d o -> o d"))
            vec(attb[:], a["L1_gnn_att_b"][layer:layer + 1, :])
            lt = ltab[layer].rearrange("(b p) d -> p b d", p=P)
            with sp.Fori(0, NSTEP) as i:
                sp.wait_ge(s2_ready, i + 1)
                sp.wait_ge(support_ready, i + 1)
                sp.dma_start(lt[:, bass.ds(i * SB, SB), :], trow[:]).then_inc(stored, 16)
            sp.wait_ge(stored, 16 * NSTEP)
        else:
            sp.wait_ge(h_ready, NSTEP)
            sp.dma_start(out[0:FULL * P, :].rearrange("(b p) d -> p b d", p=P), xall[:, 0:FULL, :]).then_inc(stored, 16)
            sp.dma_start(out[FULL * P:N, :], xall[0:REST, FULL, :]).then_inc(stored, 16)
            sp.wait_ge(stored, 32)

    SMALL = 16 * (2 + (8 if prepare else 0))

    @block.gpsimd
    def _(pool):
        if kind == "attn":
            nc.gpsimd.memset(xall[:, FULL, :], 0.0).then_inc(tail_zeroed, 1)
        if prepare:
            nc.gpsimd.memset(zeros[:], 0.0).then_inc(zeroed, 1)

    @block.scalar
    def _(act):
        if kind == "attn":
            act.wait_ge(xin, 32)

        def turn(i):
            if kind == "attn":
                wait_used(act, h_ready, i)
                nc.scalar.copy(xs[:], xall[:, bass.ds(i * SB, SB), :]).then_inc(x_copied, 1)
            if kind != "mid":
                act.wait_ge(var_ready, i + 1)
                nc.scalar.activation(st_[:, 3, :], st_[:, 2, :], ACT.Sqrt, bias=c["eps"][:, 0:1], scale=1.0 / D).then_inc(sd_ready, 1)
            if prepare:
                act.wait_ge(products, i + 1)
                wait_used(act, stored, 16 * i)
                nc.scalar.copy(trow[:, :, 0:D], view(ps[2])).then_inc(support_ready, 1)
                act.wait_ge(spread, i + 1)
                nc.scalar.copy(s1_all[:, bass.ds(i * SB, SB), :], view(psT)).then_inc(spread_read, 1)

        turns(act, 1, NSTEP, turn)

    @block.tensor
    def _(pe):
        if not prepare:
            return
        pe.wait_ge(small, SMALL)

        def turn(i):
            wait_used(pe, spread_read, i)
            if kind == "attn":
                pe.wait_ge(x_copied, i + 1)
                for j in range(SB):
                    m = nc.tensor.transpose(psT[:, j * D:(j + 1) * D], xs[:, j, :], c["ident"][:])
                m.then_inc(x_turned, 1)
                pe.wait_ge(xT_ready, i + 1)
                for j in range(SB):
                    m = nc.tensor.matmul(ps[0][:, j * D:(j + 1) * D], hT[:, j, :], wskip[:], start=True, stop=True)
                m.then_inc(skip_ready, 1)
            pe.wait_ge(h_ready, i + 1)
            for j in range(SB):
                m = nc.tensor.transpose(psT[:, j * D:(j + 1) * D], h_[:, j, :], c["ident"][:])
            m.then_inc(h_turned, 1)
            pe.wait_ge(hT_ready, i + 1)
            wait_used(pe, support_ready, i)
            for k in range(3):
                for j in range(SB):
                    m = nc.tensor.matmul(ps[k][:, j * D:(j + 1) * D], hT[:, j, :], w[:, k, :], start=True, stop=True)
            m.then_inc(products, 1)
            pe.wait_ge(dg_ready, i + 1)
            for j in range(SB):
                m = nc.tensor.matmul(psT[:, j * D:(j + 1) * D], c["ones"][:], dg[:, j, :], start=True, stop=True)
            m.then_inc(spread, 1)

        turns(pe, 1, NSTEP, turn)

    @block.vector
    def _(dve):
        dve.wait_ge(small, SMALL)
        if prepare:
            dve.wait_ge(zeroed, 1)
        K = {"attn": 19, "mid": 9, "last": 8}[kind]

        def turn(i):
            cs = Chain(dve, step, K * i)
            here = bass.ds(i * SB, SB)

            def norm(final):
                cs.then(nc.vector.tensor_reduce(st_[:, 0, :], r_[:], AX.X, ALU.add))
                cs.then(nc.vector.tensor_scalar(st_[:, 1, :], st_[:, 0, :], 1.0 / D, None, ALU.mult))
                cs.then(nc.vector.tensor_tensor(r_[:], r_[:], st_[:, 1, :].unsqueeze(2).broadcast_to(W), ALU.subtract))
                cs.then(nc.vector.tensor_tensor(sq[:], r_[:], r_[:], ALU.mult))
                nc.vector.tensor_reduce(st_[:, 2, :], sq[:], AX.X, ALU.add).then_inc(var_ready, 1)
                dve.wait_ge(sd_ready, i + 1)
                cs.then(nc.vector.reciprocal(st_[:, 0, :], st_[:, 3, :]))
                nc.vector.tensor_tensor(final, r_[:], st_[:, 0, :].unsqueeze(2).broadcast_to(W), ALU.mult).then_inc(h_ready, 1)
                dve.wait_ge(h_ready, i + 1)

            if kind == "attn":
                cs.then(nc.vector.tensor_scalar(den[:, 0, :, :], acc[:, here, CH::HW], 1e-16, None, ALU.add))
                cs.then(nc.vector.reciprocal(den[:, 1, :, :], den[:, 0, :, :]))
                cs.then(nc.vector.tensor_tensor(
                    sq[:].rearrange("p b (h d) -> p b h d", h=HEADS),
                    acc[:, here, :].rearrange("p b (h w) -> p b h w", h=HEADS)[:, :, :, 0:CH],
                    den[:, 1, :, :].unsqueeze(3).broadcast_to([P, SB, HEADS, CH]), ALU.mult))
                dve.wait_ge(x_turned, i + 1)
                nc.vector.tensor_copy(hT[:].rearrange("p b d -> p (b d)"), psT[:, 0:SB * D]).then_inc(xT_ready, 1)
                dve.wait_ge(skip_ready, i + 1)
                cs.then(nc.vector.tensor_tensor(r_[:], view(ps[0]), row(0), ALU.add))
                cs.then(nc.vector.tensor_tensor(r_[:], r_[:], sq[:], ALU.add))
                dve.wait_ge(x_copied, i + 1)
                cs.then(nc.vector.tensor_tensor(r_[:], r_[:], xs[:], ALU.add))
                norm(h_[:])
                nc.vector.tensor_scalar(xall[:, here, :], h_[:], 2.0, None, ALU.mult)
            else:
                cs.then(nc.vector.tensor_tensor(r_[:], acc[:, here, 0:D], row(0), ALU.add))
                if kind == "mid":
                    nc.vector.tensor_scalar(h_[:], r_[:], 0.0, None, ALU.max).then_inc(h_ready, 1)
                    dve.wait_ge(h_ready, i + 1)
                    nc.vector.tensor_tensor(xall[:, here, :], xall[:, here, :], h_[:], ALU.add)
                else:
                    cs.then(nc.vector.tensor_scalar(r_[:], r_[:], 0.0, None, ALU.max))
                    cs.then(nc.vector.tensor_tensor(r_[:], r_[:], xall[:, here, :], ALU.add))
                    norm(xall[:, here, :])
            if prepare:
                nc.vector.tensor_copy(acc[:, here, :], zeros[:])
                dve.wait_ge(h_turned, i + 1)
                nc.vector.tensor_copy(hT[:].rearrange("p b d -> p (b d)"), psT[:, 0:SB * D]).then_inc(hT_ready, 1)
                dve.wait_ge(products, i + 1)
                for k in range(2):
                    cs.then(nc.vector.tensor_tensor(sq[:], view(ps[k]), row(1 + k), ALU.add))
                    cs.then(nc.vector.scalar_tensor_tensor(sq[:], sq[:], 0.01, sq[:], ALU.mult, ALU.max))
                    cs.then(nc.vector.tensor_tensor(sq[:], sq[:], row(3 + k), ALU.mult))
                    if k == 0:
                        cs.then(nc.vector.tensor_reduce(s1[:, 0, :], sq[:], AX.X, ALU.add))
                        nc.vector.tensor_tensor(dg[:], c["ident"][:].unsqueeze(1).broadcast_to(W),
                                                s1[:, 0, :].unsqueeze(2).broadcast_to(W), ALU.mult).then_inc(dg_ready, 1)
                    else:
                        cs.then(nc.vector.tensor_reduce(s1[:, 1, :], sq[:], AX.X, ALU.add))
                wait_used(dve, stored, 16 * i)
                nc.vector.tensor_scalar(trow[:, :, D], s1[:, 1, :], attb[:, 0:1], None, ALU.add).then_inc(s2_ready, 1)
            assert cs.n == K, (kind, cs.n)

        turns(dve, 1, NSTEP, turn)


def convolution(nc, st, c, layer, s1_all, acc, ltab, rec1, btab):
    pre = f"c{layer}_"

    def sb(name, shape, dt=F32):
        return st.enter_context(nc.sbuf_tensor(pre + name, shape, dt))

    sem = semaphores(nc, st, pre)

    brow = sb("brow", [1, TBL], I32)
    records = sb("records", [P, MAX_TILES, R1])
    rec = [sb(f"rec{k}", [P, 4, R1]) for k in range(4)]
    g = [sb(f"g{k}", [P, 4, LR]) for k in range(4)]
    junk = sb("junk", [P, 8, P])
    z = [sb(f"z{k}", [P, 4]) for k in range(2)]
    gate_in = [sb(f"gate_in{k}", [P, 4]) for k in range(2)]
    gate = [sb(f"gate{k}", [P, 4]) for k in range(2)]
    hot = [sb(f"hot{k}", [P, 4, P]) for k in range(2)]
    psA = [st.enter_context(nc.psum_tensor(pre + f"psA{k}", [P, 512], F32)) for k in range(4)]
    table_in, records_in, rec_ready, turn_begun = sem("table_in"), sem("records_in"), sem("rec_ready"), sem("turn_begun")
    gathered = [sem(f"gathered{k}") for k in range(4)]
    z_ready, gate_in_ready, gate_ready, hot_ready, sum_ready, added = (
        sem("z_ready"), sem("gate_in_ready"), sem("gate_ready"), sem("hot_ready"), sem("sum_ready"), sem("added"))
    block = st.enter_context(nc.Block())

    @block.sync
    def _(sp):
        sp.dma_start(records[:], rec1.rearrange("(p t) d -> p t d", p=P)).then_inc(records_in, 16)
        sp.dma_start(brow[:], btab.rearrange("(o d) -> o d", o=1)).then_inc(table_in, 16)

    @block.gpsimd
    def _(pool):
        def body(q, r):
            pool.wait_ge(rec_ready, q + 1)
            if is_loop(q) or q >= 4:
                pool.wait_ge(sum_ready, q - 3)
            pool.sem_inc(turn_begun, 1)
            for j in range(4):
                nc.gpsimd.indirect_dma_start(out=g[r][:, j, :], out_offset=None, in_=ltab,
                                             in_offset=bass.IndirectOffsetOnAxis(rec[r][:, j, 0:1].bitcast(U32), 0)).then_inc(gathered[r], 16)

        run_steps(pool, 4, QUADS, body)

    @block.scalar
    def _(act):
        def take(q, r):
            nc.scalar.copy(rec[r][:], records[:, bass.ds(4 * q, 4), :]).then_inc(rec_ready, 1)

        def body(q, r):
            act.wait_ge(gate_in_ready, q + 1)
            nc.scalar.activation(gate[r % 2][:], gate_in[r % 2][:], ACT.Sigmoid).then_inc(gate_ready, 1)
            if is_loop(q) or q + 4 < QUADS:
                act.wait_ge(hot_ready, q + 1)
                take(q + 4, r)

        act.wait_ge(records_in, 16)
        for q in range(4):
            take(q, q)
        last = QUADS - 4
        with act.Fori(0, last // 4) as i:
            for r in range(4):
                body(4 * i + r, r)
        for q in range(last, QUADS):
            body(q, q % 4)

    @block.tensor
    def _(pe):
        def body(q, r):
            pe.wait_ge(hot_ready, q + 1)
            if is_loop(q) or q >= 4:
                pe.wait_ge(added, 4 * q - 11)
            for j in range(4):
                m = nc.tensor.matmul(psA[r][:, j * D:(j + 1) * D], hot[r % 2][:, j, :], g[r][:, j, 0:D], start=True, stop=True)
            m.then_inc(sum_ready, 1)

        run_steps(pe, 4, QUADS, body)

    @block.vector
    def _(dve):
        def buckets(q):
            dve.wait_ge(table_in, 16)
            _, bs = nc.values_load_multi_w_load_instructions(brow[0:1, bass.ds(4 * q, 4)], engines=[mybir.EngineType.DVE],
                                                             min_val=0, max_val=NB - 1, skip_runtime_bounds_check_because="the table is clamped to the last bucket")
            return bs

        def gates(q, r, k):
            bs = buckets(q)
            dve.wait_ge(gathered[r], 64 * k + 64)
            for j in range(4):
                s1 = s1_all[:, bass.ds(bs[j], 1), :].rearrange("p o d -> p (o d)")
                m = nc.vector.scalar_tensor_tensor(junk[:, 4 * (r % 2) + j, :], c["iota"][:], rec[r][:, j, 1:2], s1,
                                                   ALU.is_equal, ALU.mult, accum_out=z[r % 2][:, j:j + 1])
            m.then_inc(z_ready, 1)
            dve.wait_ge(z_ready, q + 1)
            nc.vector.tensor_tensor(gate_in[r % 2][:], z[r % 2][:], g[r][:, :, D], ALU.add).then_inc(gate_in_ready, 1)

        def body(q, r, k):
            if is_loop(q) or q < QUADS:
                gates(q, r, k)
            spreads = is_loop(q) or 1 <= q <= QUADS
            adds = is_loop(q) or q >= 3
            if adds:
                bs = buckets(q - 3)
                dve.wait_ge(sum_ready, q - 2)
            if spreads:
                dve.wait_ge(gate_ready, q)
            for j in range(4):
                if adds:
                    dve.wait_ge(added, 4 * (q - 3) + (j + 1))
                    at = acc[:, bass.ds(bs[j], 1), 0:D].rearrange("p o d -> p (o d)")
                    nc.vector.tensor_tensor(at, at, psA[(r - 3) % 4][:, j * D:(j + 1) * D], ALU.add).then_inc(added, 1)
                if spreads:
                    p = (r - 1) % 4
                    m = nc.vector.tensor_scalar(hot[p % 2][:, j, :], c["iota"][:], rec[p][:, j, 1:2],
                                                gate[p % 2][:, j:j + 1], ALU.is_equal, ALU.mult)
            if spreads:
                m.then_inc(hot_ready, 1)

        dve.wait_ge(table_in, 16)
        dve.sem_inc(added, 1)
        for q in range(3):
            body(q, q, 0)
        fours = (QUADS - 3) // 4
        with dve.Fori(0, fours) as i:
            for r in range(4):
                body(4 * i + (3 + r), (3 + r) % 4, i + (3 + r) // 4)
        for q in range(3 + 4 * fours, QUADS + 3):
            body(q, q % 4, q // 4)


_INS = ["x", "src", "dst", "edge_attr_64", "edge_weight", "node_vec"] + [
    f"L0_gnn_{n}" for n in ("time_w", "time_b", "Wq", "bq", "Wk", "bk", "Wv", "bv", "We", "Wskip", "bskip")] + [
    f"L1_gnn_{n}" for n in ("gcn_w", "gcn_b", "nb_w", "nb_b", "self_w", "self_b", "att_w", "att_b")]


def kernel(**inputs):
    import numpy as _np
    import concourse.bacc as _bacc
    from concourse import mybir as _mybir
    from concourse.bass_utils import run_bass_kernel_spmd as _run

    nc = _bacc.Bacc("TRN2", target_bir_lowering=False, num_devices=1)
    arrays, args = {}, {}
    for name in _INS:
        arr = _np.ascontiguousarray(inputs[name])
        arrays[f"in_{name}"] = arr
        args[name] = nc.dram_tensor(f"in_{name}", arr.shape, _mybir.dt.from_np(arr.dtype), kind="ExternalInput").ap()
    out = nc.dram_tensor("out", (N, D), _mybir.dt.float32, kind="ExternalOutput").ap()
    build(nc, args, out)
    r = _run(nc, [arrays], core_ids=[0])
    return r.results[0]["out"]
```
